# Optimizing a Trainium2 kernel written in Bass

```python
import numpy as np
import jax
import jax.numpy as jnp

def _softmax(x, axis=-1):
    return jax.nn.softmax(x, axis=axis)

def _gelu(x):
    return jax.nn.gelu(x, approximate=True)

def _silu(x):
    return jax.nn.silu(x)

def _sigmoid(x):
    return jax.nn.sigmoid(x)

def _layernorm(x, axis=-1, eps=1e-05):
    m = jnp.mean(x, axis=axis, keepdims=True)
    v = jnp.var(x, axis=axis, keepdims=True)
    return (x - m) / jnp.sqrt(v + eps)

def _scatter_add(tgt, idx, src, axis=0):
    return tgt.at[idx].add(src)

def _segment_sum(src, seg, n):
    return jax.ops.segment_sum(src, seg, n)
kernel_name = 'mk_gnn_preln_d2_gnn_r8_59b4fa'

def setup_inputs(seed: int=0):
    np.random.seed(seed)
    _w = jnp.asarray

    def _rec_inputs():
        import jax
        import jax.numpy as jnp
        _gk = jax.random.key(seed)
        x = -0.000202 + 1 * jax.random.normal(jax.random.fold_in(_gk, 1), (6250, 128), jnp.float32)
        _s = jax.random.randint(jax.random.fold_in(_gk, 2), (50000,), 0, 6250, jnp.int32)
        _d = jax.random.randint(jax.random.fold_in(_gk, 3), (50000,), 0, 6250, jnp.int32)
        _loop = jnp.arange(6250, dtype=jnp.int32)
        src = jnp.concatenate([_s, _d, _loop])
        dst = jnp.concatenate([_d, _s, _loop])
        _o = jnp.argsort(dst, stable=True)
        src = src[_o]
        dst = dst[_o]
        edge_type_16 = jax.random.randint(jax.random.fold_in(_gk, 12), (106250,), 0, 16, jnp.int32)
        return (x, src, dst, edge_type_16)
    x, src, dst, edge_type_16 = _rec_inputs()

    def _L0_gnn_setup():
        import jax, jax.numpy as jnp
        import numpy as np
        N_NODES = 6250

        def _gnn_layer(x, W, b, src, dst):
            msg = x[src] @ W.T + b
            summed = jax.ops.segment_sum(msg, dst, num_segments=N_NODES)
            cnt = jax.ops.segment_sum(jnp.ones((src.shape[0],), msg.dtype), dst, num_segments=N_NODES)
            return summed / jnp.maximum(cnt, 1.0)[:, None]
        key = jax.random.key(seed)
        k1, k2, k3, k4, k5, k6 = jax.random.split(key, 6)
        in_c, hid_c, out_c = (128, 128, 128)
        E = 100000
        x = jax.random.normal(k1, (N_NODES, in_c), dtype=jnp.float32)
        edge_index = jax.random.randint(k2, (2, E), 0, N_NODES, dtype=jnp.int64)
        s1 = 1.0 / np.sqrt(in_c)
        s2 = 1.0 / np.sqrt(hid_c)
        W1 = jax.random.uniform(k3, (hid_c, in_c), jnp.float32, -s1, s1)
        b1 = jax.random.uniform(k4, (hid_c,), jnp.float32, -s1, s1)
        W2 = jax.random.uniform(k5, (out_c, hid_c), jnp.float32, -s2, s2)
        b2 = jax.random.uniform(k6, (out_c,), jnp.float32, -s2, s2)
        return {'x': x, 'edge_index': edge_index, 'W1': W1, 'b1': b1, 'W2': W2, 'b2': b2}
    _L0_gnn_all = _L0_gnn_setup()
    _L0_gnn_in = {k: v for k, v in _L0_gnn_all.items() if k in ('W1', 'b1', 'W2', 'b2')}
    del _L0_gnn_all

    def _L1_gnn_setup():
        import jax, jax.numpy as jnp
        import numpy as np
        N, H = (6250, 128)
        E = 100000
        ETD = 32
        NUM_ET = 16
        LN_EPS = 1e-05
        key = jax.random.key(seed)
        ks = jax.random.split(key, 9)
        x = jax.random.normal(ks[0], (N, H), dtype=jnp.float32)
        edge_index = jax.random.randint(ks[1], (2, E), 0, N, dtype=jnp.int64)
        edge_type = jax.random.randint(ks[2], (E,), 0, NUM_ET, dtype=jnp.int64)
        edge_emb_W = jax.random.normal(ks[3], (NUM_ET, ETD), dtype=jnp.float32)
        lim_msg = 1.0 / np.sqrt(H + ETD)
        msg_W = jax.random.uniform(ks[4], (H, H + ETD), jnp.float32, -lim_msg, lim_msg)
        msg_b = jax.random.uniform(ks[5], (H,), jnp.float32, -lim_msg, lim_msg)
        lim_upd = 1.0 / np.sqrt(H)
        upd_W = jax.random.uniform(ks[6], (H, H), jnp.float32, -lim_upd, lim_upd)
        upd_b = jax.random.uniform(ks[7], (H,), jnp.float32, -lim_upd, lim_upd)
        ln_g = jnp.ones((H,), jnp.float32)
        ln_b = jnp.zeros((H,), jnp.float32)
        return {'x': x, 'edge_index': edge_index, 'edge_type': edge_type, 'edge_emb_W': edge_emb_W, 'msg_W': msg_W, 'msg_b': msg_b, 'upd_W': upd_W, 'upd_b': upd_b, 'ln_g': ln_g, 'ln_b': ln_b}
    _L1_gnn_all = _L1_gnn_setup()
    _L1_gnn_in = {k: v for k, v in _L1_gnn_all.items() if k in ('edge_emb_W', 'msg_W', 'msg_b', 'upd_W', 'upd_b', 'ln_g', 'ln_b')}
    del _L1_gnn_all
    return {'x': x, 'src': src, 'dst': dst, 'edge_type_16': edge_type_16, 'L0_gnn_W1': _L0_gnn_in['W1'], 'L0_gnn_b1': _L0_gnn_in['b1'], 'L0_gnn_W2': _L0_gnn_in['W2'], 'L0_gnn_b2': _L0_gnn_in['b2'], 'L1_gnn_edge_emb_W': _L1_gnn_in['edge_emb_W'], 'L1_gnn_msg_W': _L1_gnn_in['msg_W'], 'L1_gnn_msg_b': _L1_gnn_in['msg_b'], 'L1_gnn_upd_W': _L1_gnn_in['upd_W'], 'L1_gnn_upd_b': _L1_gnn_in['upd_b'], 'L1_gnn_ln_g': _L1_gnn_in['ln_g'], 'L1_gnn_ln_b': _L1_gnn_in['ln_b']}

def reference(x, src, dst, edge_type_16, L0_gnn_W1, L0_gnn_b1, L0_gnn_W2, L0_gnn_b2, L1_gnn_edge_emb_W, L1_gnn_msg_W, L1_gnn_msg_b, L1_gnn_upd_W, L1_gnn_upd_b, L1_gnn_ln_g, L1_gnn_ln_b):
    import jax
    import jax.numpy as jnp

    def _L0_gnn_ref(x, edge_index, W1, b1, W2, b2):
        import jax, jax.numpy as jnp
        import numpy as np
        N_NODES = 6250

        def _gnn_layer(x, W, b, src, dst):
            msg = x[src] @ W.T + b
            summed = jax.ops.segment_sum(msg, dst, num_segments=N_NODES)
            cnt = jax.ops.segment_sum(jnp.ones((src.shape[0],), msg.dtype), dst, num_segments=N_NODES)
            return summed / jnp.maximum(cnt, 1.0)[:, None]
        src, dst = (edge_index[0], edge_index[1])
        h = _gnn_layer(x, W1, b1, src, dst)
        h = jax.nn.relu(h)
        out = _gnn_layer(h, W2, b2, src, dst)
        return out

    def _L1_gnn_ref(x, edge_index, edge_type, edge_emb_W, msg_W, msg_b, upd_W, upd_b, ln_g, ln_b):
        import jax, jax.numpy as jnp
        import numpy as np
        N, H = (6250, 128)
        E = 100000
        ETD = 32
        NUM_ET = 16
        LN_EPS = 1e-05
        src = edge_index[0]
        dst = edge_index[1]
        et = edge_emb_W[edge_type]
        m_in = jnp.concatenate([x[src], et], axis=-1)
        m = jax.nn.relu(m_in @ msg_W.T + msg_b)
        agg = jax.ops.segment_sum(m, dst, num_segments=x.shape[0])
        deg = jax.ops.segment_sum(jnp.ones_like(dst, dtype=x.dtype), dst, num_segments=x.shape[0])
        agg = agg / jnp.clip(deg, 1.0)[:, None]
        out = agg @ upd_W.T + upd_b
        h = x + out
        mu = jnp.mean(h, axis=-1, keepdims=True)
        var = jnp.mean((h - mu) ** 2, axis=-1, keepdims=True)
        return (h - mu) * jax.lax.rsqrt(var + LN_EPS) * ln_g + ln_b
    edge_index = jnp.stack([src, dst])
    h = jnp.maximum(_layernorm(x, axis=-1), 0.0)
    x = x + _L0_gnn_ref(h, edge_index, L0_gnn_W1, L0_gnn_b1, L0_gnn_W2, L0_gnn_b2)
    h = jnp.maximum(_layernorm(x, axis=-1), 0.0)
    x = x + _L1_gnn_ref(h, edge_index, edge_type_16, L1_gnn_edge_emb_W, L1_gnn_msg_W, L1_gnn_msg_b, L1_gnn_upd_W, L1_gnn_upd_b, L1_gnn_ln_g, L1_gnn_ln_b)
    return x

_drawn_inputs = setup_inputs


def setup_inputs(seed=0):
    import zlib

    import numpy as np

    out = dict(_drawn_inputs(seed))
    spreads = {'L1_gnn_ln_g': (1.0, 0.2), 'L1_gnn_ln_b': (0.0, 0.1)}
    factors = {'L1_gnn_msg_b': 3.513}
    for name, (base, spread) in spreads.items():
        noise = np.random.default_rng([zlib.crc32(name.encode()), seed]).standard_normal(out[name].shape)
        drawn = base * np.exp(spread * noise) if base else spread * noise
        out[name] = jnp.asarray(drawn.astype(out[name].dtype))
    for name, factor in factors.items():
        out[name] = (out[name] * factor).astype(out[name].dtype)
    return out
```

```python
import concourse.bass as bass
from concourse import mybir
from contextlib import ExitStack

P = 128


def gnn_program(nc, N, E, GROUPS, x, src, dst, first_dst, etype, W1T, b1, W2T, b2, embT, msgWT, msg_b,
                updWT, upd_b, ln_g, ln_b, out):
    fp32 = mybir.dt.float32
    i32 = mybir.dt.int32
    ALU = mybir.AluOpType
    ACT = mybir.ActivationFunctionType
    AX = mybir.AxisListType

    F = x.shape[1]
    TILES = x.shape[0] // P
    ETD, TYPES = embT.shape
    C = 8
    GE = C * P
    SLOTS = 2
    ITERS = GROUPS // SLOTS
    WINDOWS = TILES + 1
    COLS = WINDOWS * P
    HALVES = ((0, 4), (4, 3))
    STEP = 7
    STEPS = TILES // STEP
    EPS = 1e-5
    assert TILES == STEP * STEPS and GROUPS == SLOTS * ITERS and N + P <= COLS

    ctx = ExitStack()
    with ctx:
        def sb(name, shape, dt=fp32):
            return ctx.enter_context(nc.sbuf_tensor(name, shape, dt))

        def sem(name):
            return ctx.enter_context(nc.semaphore(name))

        def sems(name, n):
            return [sem(f"{name}{k}") for k in range(n)]

        tables = [nc.dram_tensor(f"table{k}", (TILES * P, F), fp32, kind="Internal").ap() for k in range(3)]
        table_v = [t.rearrange("(t p) f -> p t f", p=P) for t in tables]
        x_v = x.rearrange("(t p) f -> p t f", p=P)
        out_v = out.rearrange("(t p) f -> p t f", p=P)

        src_all = sb("src_all", [P, (GROUPS + SLOTS) * C], i32)
        dst_all = sb("dst_all", [P, GROUPS * C], i32)
        base_all = sb("base_all", [P, GROUPS], i32)
        rel = sb("rel", [P, GROUPS * C])
        far = sb("far", [P, GROUPS * C])
        far_max = sb("far_max", [P, 1])
        far_one = sb("far_one", [P, 1])
        flag = sb("flag", [1, 1], i32)
        fb_idx_cols = sb("fb_idx_cols", [P, C], i32)
        far_w = sb("far_w", [P, C])
        columns = sb("columns", [P, P])
        type_no = sb("type_no", [TYPES, 1])
        ones = sb("ones", [P, P])
        ident = sb("ident", [P, P])
        eps = sb("eps", [P, 1])
        w1 = sb("w1", [P, F])
        w2 = sb("w2", [P, F])
        wm = sb("wm", [P, F])
        wt = sb("wt", [ETD, F])
        wu = sb("wu", [P, F])
        emb = sb("emb", [ETD, TYPES])
        rows_b = sb("rows_b", [1, 4, F])
        g_all = sb("g_all", [P, F])
        b_all = sb("b_all", [P, F])
        type_rows = sb("type_rows", [TYPES, F])
        idx = [sb(f"idx{s}", [P, C], i32) for s in range(SLOTS)]
        rows = [sb(f"rows{s}", [P, C, F]) for s in range(SLOTS)]
        hot = [sb(f"hot{s}", [P, C, P]) for s in range(SLOTS)]
        types_in = [sb(f"types_in{s}", [TYPES, GE], i32) for s in range(SLOTS)]
        types_hot = [sb(f"types_hot{s}", [TYPES, GE]) for s in range(SLOTS)]
        msgs = [sb(f"msgs{s}", [P, C, F]) for s in range(SLOTS)]
        agg = sb("agg", [P, COLS])
        cnt = sb("cnt", [P, COLS])
        tmp = cnt[:, 0:GROUPS * C]
        rinv = sb("rinv", [P, COLS])
        xres = sb("xres", [P, TILES, F])
        hres = sb("hres", [P, TILES, F])
        stats = sb("stats", [P, TILES, 6])
        mean = sb("mean", [P, TILES])
        var = sb("var", [P, TILES])
        std = sb("std", [P, TILES])
        rstd = sb("rstd", [P, TILES])
        nmr = sb("nmr", [P, TILES])
        mean_T = [sb(f"mean_T{h}", [P, n * P]) for h, (_, n) in enumerate(HALVES)]
        has_in = [sb(f"has_in{h}", [1, n * P]) for h, (_, n) in enumerate(HALVES)]
        hslot = [sb(f"hslot{h}", [P, n, F]) for h, (_, n) in enumerate(HALVES)]
        oslot = [sb(f"oslot{h}", [P, n, F]) for h, (_, n) in enumerate(HALVES)]

        banks = ctx.enter_context(nc.psum_tensor("banks", [P, 8, 512], fp32))
        sum_ps = [banks[:, s, 0:P] for s in range(SLOTS)]
        cnt_ps = [banks[:, 2 + s, 0:P] for s in range(SLOTS)]
        type_ps = [banks[:, 4 + 2 * s:6 + 2 * s, :].rearrange("p b (c f) -> p (b c) f", f=F) for s in range(SLOTS)]
        post_ps = [banks[:, 4 + h, :].rearrange("p (t f) -> p t f", f=F) for h in range(2)]
        tr_ps = [banks[:, 6 + h, :] for h in range(2)]
        setup_ps = banks[:, 7, :]

        edges_in = sem("edges_in")
        x_in = sem("x_in")
        weights_in = sem("weights_in")
        consts = sem("consts")
        dve_step = sem("dve_step")
        far_ready = sem("far_ready")
        far_known = sem("far_known")
        setup_done = sem("setup_done")
        type_rows_ready = sem("type_rows_ready")
        types_loaded = sems("types_loaded", SLOTS)
        types_hot_ready = sems("types_hot_ready", SLOTS)
        types_done = sems("types_done", SLOTS)
        pre_ready = sems("pre_ready", SLOTS)
        msgs_ready = sems("msgs_ready", SLOTS)
        idx_ready = sems("idx_ready", SLOTS)
        gathered = sems("gathered", SLOTS)
        hot_ready = sems("hot_ready", SLOTS)
        summed = sems("summed", SLOTS)
        added = sem("added")
        counted = sem("counted")
        fb_idx = sem("fb_idx")
        fb_gathered = sem("fb_gathered")
        fb_types_in = sem("fb_types_in")
        fb_types_hot = sem("fb_types_hot")
        fb_types_done = sem("fb_types_done")
        fb_pre = sem("fb_pre")
        fb_msgs = sem("fb_msgs")
        fb_hot = sem("fb_hot")
        fb_summed = sem("fb_summed")
        fb_added = sem("fb_added")
        mean_ready = sems("mean_ready", 2)
        post_done = sems("post_done", 2)
        post_read = sems("post_read", 2)
        stats_ready = sem("stats_ready")
        std_ready = sem("std_ready")
        norm_ready = sem("norm_ready")
        h_ready = sems("h_ready", 2)
        h_copied = sems("h_copied", 2)
        tr_done = sems("tr_done", 2)
        tr_read = sems("tr_read", 2)
        y_done = sems("y_done", 2)
        scaled = sems("scaled", 2)
        rows_ready = sems("rows_ready", 2)
        stored = sems("stored", 2)

        EDGE_LOADS = 4 * 16
        WEIGHT_LOADS = 12 * 16
        CONSTS = 8
        LAYERS = 3
        FB_ALL = GROUPS * WINDOWS

        block = ctx.enter_context(nc.Block())

        def loop(eng, n, step, peel=False):
            if peel:
                step(0, True)
            with eng.Fori(1 if peel else 0, n) as i:
                step(i, False)

        class Steps:

            def __init__(self, eng):
                self.eng, self.base, self.n = eng, 0, 0

            def done(self, ins):
                ins.then_inc(dve_step, 1)
                self.n += 1

            def wait(self):
                self.eng.wait_ge(dve_step, self.base + self.n)

            def loop(self, n, per, step, peel=False):
                start = self.base + self.n

                def one(i, first):
                    self.base, self.n = i * per + start, 0
                    step(i, first)
                    assert self.n == per
                loop(self.eng, n, one, peel)
                self.base, self.n = start + n * per, 0

        def tiles(i, h):
            t0, n = HALVES[h]
            return bass.ds(i * STEP + t0, n)

        def nodes(i, h):
            t0, n = HALVES[h]
            return bass.ds(i * (STEP * P) + t0 * P, n * P)

        @block.sync
        def _(sp):
            sp.dma_start(xres[:, :, :], x_v).then_inc(x_in, 16)
            sp.dma_start(src_all[:, 0:GROUPS * C], src).then_inc(edges_in, 16)
            sp.dma_start(src_all[:, GROUPS * C:], src[:, 0:SLOTS * C]).then_inc(edges_in, 16)
            sp.dma_start(dst_all[:, :], dst).then_inc(edges_in, 16)
            sp.dma_start(base_all[:, :], first_dst.partition_broadcast(P)).then_inc(edges_in, 16)
            for to, w in ((w1, W1T), (w2, W2T), (wm, msgWT[0:F, :]), (wt, msgWT[F:F + ETD, :]), (wu, updWT), (emb, embT)):
                sp.dma_start(to[:, :], w).then_inc(weights_in, 16)
            for k, b in enumerate((b1, b2, msg_b, upd_b)):
                sp.dma_start(rows_b[0:1, k, :], b.rearrange("(a f) -> a f", a=1)).then_inc(weights_in, 16)
            sp.dma_start(g_all[:, :], ln_g.partition_broadcast(P)).then_inc(weights_in, 16)
            sp.dma_start(b_all[:, :], ln_b.partition_broadcast(P)).then_inc(weights_in, 16)

            def store(phase, to):
                def step(i, first):
                    for h, (_, n) in enumerate(HALVES):
                        sp.wait_ge(rows_ready[h], i + (phase * STEPS + 1))
                        sp.dma_start(to[:, tiles(i, h), :], oslot[h][:, :, :]).then_inc(stored[h], 16)
                loop(sp, STEPS, step)

            for phase, to in enumerate(table_v):
                store(phase, to)

            def load_types(to, g, done):
                sp.dma_start(to[:, :], etype[bass.ds(g, 1), :, :].rearrange("a r e -> (a r) e")).then_inc(done, 16)

            def types_step(i, first):
                for s in range(SLOTS):
                    if not first:
                        sp.wait_ge(types_hot_ready[s], i)
                    load_types(types_in[s], i * SLOTS + s, types_loaded[s])
            loop(sp, ITERS, types_step, peel=True)
            sp.wait_ge(far_known, 1)
            with sp.If(sp.value_load(flag[0:1, 0:1], min_val=0, max_val=P) > 0):
                sp.wait_ge(added, LAYERS * GROUPS)
                def fb_step(g, first):
                    if not first:
                        sp.wait_ge(fb_types_hot, g)
                    load_types(types_in[0], g, fb_types_in)
                loop(sp, GROUPS, fb_step, peel=True)
            store(LAYERS, out_v)
            for h in range(2):
                sp.wait_ge(stored[h], 16 * (LAYERS + 1) * STEPS)

        @block.gpsimd
        def _(pool):
            nc.gpsimd.iota(columns[:, :], [[1, P]], base=0, channel_multiplier=0,
                           allow_small_or_imprecise_dtypes=True).then_inc(consts, 1)
            nc.gpsimd.iota(type_no[:, :], [[0, 1]], base=0, channel_multiplier=1,
                           allow_small_or_imprecise_dtypes=True).then_inc(consts, 1)
            nc.gpsimd.memset(ones[:, :], 1.0).then_inc(consts, 1)
            nc.gpsimd.memset(eps[:, :], EPS).then_inc(consts, 1)
            nc.gpsimd.memset(ident[:, :], 0.0).then_inc(consts, 1)
            pool.wait_ge(consts, 5)
            nc.gpsimd.affine_select(out=ident[:, :], in_=ident[:, :], compare_op=ALU.not_equal, fill=1.0,
                                    base=0, pattern=[[-1, P]], channel_multiplier=1).then_inc(consts, CONSTS - 5)

            def table_complete(layer):
                for h in range(2):
                    pool.wait_ge(stored[h], 16 * STEPS * (layer + 1))

            def gather(layer, to, cols, done):
                for c in range(C):
                    nc.gpsimd.indirect_dma_start(
                        out=to[:, c, :], out_offset=None, in_=tables[layer],
                        in_offset=bass.IndirectOffsetOnAxis(ap=cols[:, c:c + 1], axis=0)).then_inc(done, 16)

            for layer in range(LAYERS):
                def step(i, first):
                    k = i + layer * ITERS
                    if layer > 0 and not first:
                        k = pool.snap(pool.to_reg(k))
                    k1 = pool.snap(pool.to_reg(k + 1))
                    for s in range(SLOTS):
                        table_complete(layer)
                        pool.wait_ge(idx_ready[s], k1)
                        if layer == 2 and not first:
                            pool.wait_ge(pre_ready[s], i)
                        elif layer > 0 or not first:
                            pool.wait_ge(summed[s], k)
                        gather(layer, rows[s], idx[s], gathered[s])
                loop(pool, ITERS, step, peel=layer != 1)

                if layer == 0:
                    pool.wait_ge(far_known, 1)
                    far_n = pool.value_load(flag[0:1, 0:1], min_val=0, max_val=P)
                with pool.If(far_n > 0):
                    def fb_step(g, first):
                        g1 = pool.snap(pool.to_reg(g + (layer * GROUPS + 1)))
                        table_complete(layer)
                        pool.wait_ge(fb_idx, g1)
                        gather(layer, rows[0], fb_idx_cols, fb_gathered)
                    loop(pool, GROUPS, fb_step)

                if layer == 1:
                    def keep(i, first):
                        for h in range(2):
                            pool.wait_ge(h_ready[h], i + 1)
                            nc.gpsimd.tensor_copy(hres[:, tiles(i, h), :], hslot[h][:, :, :]).then_inc(h_copied[h], 1)
                    loop(pool, STEPS, keep)

            def residual(i, first):
                for h in range(2):
                    pool.wait_ge(scaled[h], i + 1)
                    nc.gpsimd.tensor_tensor(oslot[h][:, :, :], oslot[h][:, :, :], xres[:, tiles(i, h), :],
                                            ALU.add).then_inc(rows_ready[h], 1)
            loop(pool, STEPS, residual)

        @block.scalar
        def _(act):
            def normalise(i, h, to, func, inp):
                t0, n = HALVES[h]
                for j in range(n):
                    t = bass.ds(i * STEP + (t0 + j), 1)
                    last = nc.scalar.activation(to[h][:, j:j + 1, :], inp[:, t, :], func,
                                                bias=nmr[:, t], scale=rstd[:, t])
                return last

            def make_std(k):
                act.wait_ge(stats_ready, k)
                nc.scalar.activation(std[:, :], var[:, :], ACT.Sqrt, bias=eps[:, 0:1]).then_inc(std_ready, 1)
                act.wait_ge(norm_ready, k)

            def oslot_free(phase, i, h, first):
                if phase > 0 or not first:
                    act.wait_ge(stored[h], i * 16 + 16 * STEPS * phase)

            act.wait_ge(consts, CONSTS)
            make_std(1)

            def first_rows(i, first):
                for h in range(2):
                    oslot_free(0, i, h, first)
                    normalise(i, h, oslot, ACT.Relu, xres).then_inc(rows_ready[h], 1)
            loop(act, STEPS, first_rows, peel=True)

            def layer0_rows(i, first):
                for h in range(2):
                    act.wait_ge(post_done[h], i + 1)
                    oslot_free(1, i, h, first)
                    nc.scalar.activation(oslot[h][:, :, :], post_ps[h][:, 0:HALVES[h][1], :], ACT.Relu)\
                        .then_inc(rows_ready[h], 1)
            loop(act, STEPS, layer0_rows)

            make_std(2)

            def layer1_rows(i, first):
                for h in range(2):
                    if not first:
                        act.wait_ge(tr_done[h], i)
                        act.wait_ge(h_copied[h], i)
                    normalise(i, h, hslot, ACT.Relu, xres).then_inc(h_ready[h], 1)
                for h in range(2):
                    act.wait_ge(y_done[h], i + 1)
                    oslot_free(2, i, h, first)
                    nc.scalar.activation(oslot[h][:, :, :], post_ps[h][:, 0:HALVES[h][1], :], ACT.Copy)\
                        .then_inc(rows_ready[h], 1)
            loop(act, STEPS, layer1_rows, peel=True)

            def messages(i, first):
                for s in range(SLOTS):
                    act.wait_ge(pre_ready[s], i + 1)
                    nc.scalar.activation(msgs[s][:, :, :], msgs[s][:, :, :], ACT.Relu).then_inc(msgs_ready[s], 1)
            loop(act, ITERS, messages)
            act.wait_ge(far_known, 1)
            with act.If(act.value_load(flag[0:1, 0:1], min_val=0, max_val=P) > 0):
                def fb_step(g, first):
                    act.wait_ge(fb_pre, g + 1)
                    nc.scalar.activation(msgs[0][:, :, :], msgs[0][:, :, :], ACT.Relu).then_inc(fb_msgs, 1)
                loop(act, GROUPS, fb_step)

            make_std(3)

            def last_rows(i, first):
                for h in range(2):
                    if not first:
                        act.wait_ge(scaled[h], i)
                    normalise(i, h, hslot, ACT.Identity, hres).then_inc(h_ready[h], 1)
            loop(act, STEPS, last_rows, peel=True)

        @block.tensor
        def _(pe):
            pe.wait_ge(weights_in, WEIGHT_LOADS)
            pe.wait_ge(consts, CONSTS)
            nc.tensor.matmul(setup_ps[0:TYPES, 0:F], emb[:, :], wt[:, :], start=True, stop=True).then_inc(setup_done, 1)
            pe.wait_ge(far_ready, 1)
            nc.tensor.matmul(setup_ps[0:1, F:F + 1], far_one[:, 0:1], ones[:, 0:1], start=True, stop=True)\
                .then_inc(setup_done, 1)

            def window_sum(values, s):
                for c in range(C):
                    last = nc.tensor.matmul(sum_ps[s], values[:, c, :], hot[s][:, c, :], start=c == 0, stop=c == C - 1)
                return last

            def window_count(s):
                for c in range(C):
                    last = nc.tensor.matmul(cnt_ps[s], ones[:, :], hot[s][:, c, :], start=c == 0, stop=c == C - 1)
                return last

            def type_rows_of_group(s):
                for c in range(C):
                    last = nc.tensor.matmul(type_ps[s][:, c, :], types_hot[s][:, c * P:(c + 1) * P], type_rows[:, :],
                                            start=True, stop=True)
                return last

            far_n = None
            for layer in range(LAYERS):
                def step(i, first):
                    k = i + layer * ITERS
                    for s in range(SLOTS):
                        if layer == 2:
                            pe.wait_ge(types_hot_ready[s], i + 1)
                            if not first:
                                pe.wait_ge(pre_ready[s], i)
                            type_rows_of_group(s).then_inc(types_done[s], 1)
                        pe.wait_ge(hot_ready[s], k + 1)
                        if layer > 0 or not first:
                            pe.wait_ge(added, k * SLOTS + (s - SLOTS + 1))
                            if layer == 0:
                                pe.wait_ge(counted, k * SLOTS + (s - SLOTS + 1))
                        if layer == 0:
                            window_count(s)
                        if layer == 2:
                            pe.wait_ge(msgs_ready[s], i + 1)
                        else:
                            pe.wait_ge(gathered[s], k * (16 * C) + 16 * C)
                        window_sum(msgs[s] if layer == 2 else rows[s], s).then_inc(summed[s], 1)
                if layer == 2:
                    pe.wait_ge(type_rows_ready, 1)
                    for h in range(2):
                        pe.wait_ge(rows_ready[h], 3 * STEPS)
                loop(pe, ITERS, step, peel=layer != 1)

                if layer == 0:
                    pe.wait_ge(far_known, 1)
                    far_n = pe.value_load(flag[0:1, 0:1], min_val=0, max_val=P)
                with pe.If(far_n > 0):
                    def fb_group(g, first):
                        if layer == 2:
                            pe.wait_ge(fb_types_hot, g + 1)
                            type_rows_of_group(0).then_inc(fb_types_done, 1)

                        def fb_window(w, first):
                            if layer == 2:
                                pe.wait_ge(fb_msgs, g + 1)
                            else:
                                pe.wait_ge(fb_gathered, g * (16 * C) + 16 * C * (layer * GROUPS + 1))
                            pe.wait_ge(fb_hot, g * WINDOWS + w + (layer * FB_ALL + 1))
                            if layer == 0:
                                window_count(0)
                            window_sum(msgs[0] if layer == 2 else rows[0], 0).then_inc(fb_summed, 1)
                        loop(pe, WINDOWS, fb_window)
                    loop(pe, GROUPS, fb_group)

                def node_products(h, left, weight, bias, bias_left):
                    for j in range(HALVES[h][1]):
                        at = slice(j * P, (j + 1) * P)
                        nc.tensor.matmul(post_ps[h][:, j, :], left[h][:, at], weight[:, :], start=True, stop=False)
                        last = nc.tensor.matmul(post_ps[h][:, j, :], bias_left(h, at), rows_b[0:1, bias, :],
                                                start=False, stop=True)
                    return last

                def post(i, first):
                    for h in range(2):
                        pe.wait_ge(mean_ready[h], i * 2 + (layer * 2 * STEPS + 2) if layer < 2
                                   else i + (4 * STEPS + 1))
                        if layer == 0 and not first:
                            pe.wait_ge(rows_ready[h], i + STEPS)
                        if layer > 0 and not first:
                            pe.wait_ge(post_read[h], i + (layer - 1) * STEPS)
                        if layer == 1 and first:
                            pe.wait_ge(rows_ready[h], 2 * STEPS)
                        weight, bias = ((w1, 0), (w2, 1), (wu, 3))[layer]
                        node_products(h, mean_T, weight, bias,
                                      (lambda h, at: has_in[h][0:1, at]) if layer < 2 else (lambda h, at: ones[0:1, :]))\
                            .then_inc(post_done[h], 1)
                loop(pe, STEPS, post, peel=True)

                if layer == 1:
                    def source_part(i, first):
                        for h, (_, n) in enumerate(HALVES):
                            pe.wait_ge(h_ready[h], i + 1)
                            if not first:
                                pe.wait_ge(tr_read[h], i)
                            for j in range(n):
                                last = nc.tensor.transpose(tr_ps[h][:, j * P:(j + 1) * P], hslot[h][:, j, :], ident[:, :])
                            last.then_inc(tr_done[h], 1)
                        for h in range(2):
                            pe.wait_ge(tr_read[h], i + 1)
                            if not first:
                                pe.wait_ge(rows_ready[h], i + 2 * STEPS)
                            node_products(h, mean_T, wm, 2, lambda h, at: ones[0:1, :]).then_inc(y_done[h], 1)
                    loop(pe, STEPS, source_part, peel=True)

        @block.vector
        def _(dve):
            steps = Steps(dve)

            def tile_stats(source, i, h):
                t0, n = HALVES[h]
                for j in range(n):
                    t = bass.ds(i * STEP + (t0 + j), 1)
                    last = nc.vector.bn_stats(stats[:, t, :], source[:, t, :])
                return last

            def mean_and_var():
                steps.wait()
                steps.done(nc.vector.tensor_tensor(mean[:, :], stats[:, :, 1], stats[:, :, 4], ALU.add))
                steps.done(nc.vector.tensor_tensor(std[:, :], stats[:, :, 1], stats[:, :, 4], ALU.subtract))
                steps.done(nc.vector.tensor_tensor(var[:, :], stats[:, :, 2], stats[:, :, 5], ALU.add))
                steps.wait()
                steps.done(nc.vector.tensor_single_scalar(mean[:, :], mean[:, :], 0.5, op=ALU.mult))
                steps.done(nc.vector.scalar_tensor_tensor(out=std[:, :], in0=std[:, :], scalar=0.25, in1=std[:, :],
                                                          op0=ALU.mult, op1=ALU.mult))
                steps.wait()
                nc.vector.scalar_tensor_tensor(out=var[:, :], in0=var[:, :], scalar=1.0 / F, in1=std[:, :],
                                               op0=ALU.mult, op1=ALU.add).then_inc(stats_ready, 1)

            def make_norm(k):
                dve.wait_ge(std_ready, k)
                steps.done(nc.vector.reciprocal(rstd[:, :], std[:, :]))
                steps.wait()
                nc.vector.scalar_tensor_tensor(out=nmr[:, :], in0=mean[:, :], scalar=-1.0, in1=rstd[:, :],
                                               op0=ALU.mult, op1=ALU.mult).then_inc(norm_ready, 1)

            dve.wait_ge(x_in, 16)

            def x_stats(i, first):
                for h in range(2):
                    steps.done(tile_stats(xres, i, h))
            steps.loop(STEPS, 2, x_stats)
            mean_and_var()

            dve.wait_ge(edges_in, EDGE_LOADS)
            dve.wait_ge(consts, CONSTS)
            for s in range(SLOTS):
                nc.vector.tensor_copy(idx[s][:, :], src_all[:, s * C:(s + 1) * C]).then_inc(idx_ready[s], 1)
            make_norm(1)
            per_group = lambda a: a[:, :].rearrange("p (g c) -> p g c", c=C)
            steps.done(nc.vector.tensor_tensor(per_group(rel), per_group(dst_all),
                                               base_all[:, :].unsqueeze(2).broadcast_to([P, GROUPS, C]), ALU.subtract))
            steps.wait()
            steps.done(nc.vector.tensor_single_scalar(tmp, rel[:, :], 0.0, op=ALU.is_lt))
            steps.wait()
            steps.done(nc.vector.scalar_tensor_tensor(out=far[:, :], in0=rel[:, :], scalar=float(P - 1), in1=tmp,
                                                      op0=ALU.is_gt, op1=ALU.max))
            steps.wait()
            steps.done(nc.vector.scalar_tensor_tensor(out=tmp, in0=dst_all[:, :], scalar=1.0, in1=far[:, :],
                                                      op0=ALU.add, op1=ALU.mult))
            steps.wait()
            steps.done(nc.vector.tensor_single_scalar(far[:, :], tmp, -1.0, op=ALU.add))
            steps.wait()
            steps.done(nc.vector.reduce_max(far_max[:, :], far[:, :], axis=AX.X))
            steps.wait()
            nc.vector.tensor_single_scalar(far_one[:, :], far_max[:, :], 0.0, op=ALU.is_ge).then_inc(far_ready, 1)
            dve.wait_ge(setup_done, 2)
            nc.vector.tensor_copy(type_rows[:, :], setup_ps[0:TYPES, 0:F]).then_inc(type_rows_ready, 1)
            nc.vector.tensor_copy(flag[0:1, 0:1], setup_ps[0:1, F:F + 1]).then_inc(far_known, 1)
            steps.done(nc.vector.memset(cnt[:, :], 0.0))
            dve.wait_ge(far_known, 1)
            far_n = dve.value_load(flag[0:1, 0:1], min_val=0, max_val=P)

            columns_of_chunks = columns[:, :].unsqueeze(1).broadcast_to([P, C, P])

            def make_types_hot(s, to):
                return nc.vector.tensor_scalar(types_hot[s][:, :], types_in[s][:, :], type_no[:, 0:1], None, ALU.is_equal)

            for layer in range(LAYERS):
                for h in range(2):
                    if layer > 0:
                        dve.wait_ge(mean_ready[h], layer * 2 * STEPS)
                steps.done(nc.vector.memset(agg[:, :], 0.0))
                steps.wait()

                def group(i, first):
                    k = i + layer * ITERS
                    for s in range(SLOTS):
                        g = i * SLOTS + s
                        if layer > 0 or not first:
                            dve.wait_ge(summed[s], k)
                        nc.vector.tensor_tensor(hot[s][:, :, :], columns_of_chunks,
                                                rel[:, bass.ds(g * C, C)].unsqueeze(2).broadcast_to([P, C, P]),
                                                ALU.is_equal).then_inc(hot_ready[s], 1)
                        if layer == 2:
                            dve.wait_ge(types_loaded[s], i * 16 + 16)
                            if not first:
                                dve.wait_ge(types_done[s], i)
                            make_types_hot(s, types_hot[s]).then_inc(types_hot_ready[s], 1)
                        base = dve.value_load(base_all[0:1, bass.ds(g, 1)], min_val=0, max_val=N)
                        dve.wait_ge(gathered[s], k * (16 * C) + 16 * C)
                        nc.vector.tensor_copy(idx[s][:, :], src_all[:, bass.ds(g * C + SLOTS * C, C)])\
                            .then_inc(idx_ready[s], 1)
                        if layer == 2:
                            dve.wait_ge(types_done[s], i + 1)
                            nc.vector.tensor_tensor(msgs[s][:, :, :], type_ps[s], rows[s][:, :, :], ALU.add)\
                                .then_inc(pre_ready[s], 1)
                        dve.wait_ge(summed[s], k + 1)
                        window = bass.ds(base, P)
                        if layer > 0 or not first or s > 0:
                            dve.wait_ge(added, k * SLOTS + s)
                        nc.vector.tensor_tensor(agg[:, window], agg[:, window], sum_ps[s], ALU.add).then_inc(added, 1)
                        if layer == 0:
                            if not first or s > 0:
                                dve.wait_ge(counted, k * SLOTS + s)
                            nc.vector.tensor_tensor(cnt[:, window], cnt[:, window], cnt_ps[s], ALU.add).then_inc(counted, 1)
                loop(dve, ITERS, group, peel=layer != 1)
                dve.wait_ge(added, (layer + 1) * GROUPS)
                dve.wait_ge(counted, GROUPS)
                with dve.If(far_n > 0):
                    def fb_group(g, first):
                        nc.vector.tensor_copy(fb_idx_cols[:, :], src_all[:, bass.ds(g * C, C)]).then_inc(fb_idx, 1)
                        if layer == 2:
                            dve.wait_ge(fb_types_in, g * 16 + 16)
                            make_types_hot(0, types_hot[0]).then_inc(fb_types_hot, 1)
                        dve.wait_ge(fb_gathered, g * (16 * C) + 16 * C * (layer * GROUPS + 1))
                        if layer == 2:
                            dve.wait_ge(fb_types_done, g + 1)
                            nc.vector.tensor_tensor(msgs[0][:, :, :], type_ps[0], rows[0][:, :, :], ALU.add).then_inc(fb_pre, 1)

                        def fb_window(w, first):
                            at = g * WINDOWS + w + (layer * FB_ALL + 1)
                            dve.wait_ge(fb_added, g * (3 * WINDOWS + 1) + w * 3 + (layer * (3 * FB_ALL + GROUPS) + 1))
                            nc.vector.tensor_tensor(hot[0][:, :, :], columns_of_chunks,
                                                    far_w[:, :].unsqueeze(2).broadcast_to([P, C, P]),
                                                    ALU.is_equal).then_inc(fb_hot, 1)
                            dve.wait_ge(fb_hot, at)
                            nc.vector.tensor_single_scalar(far_w[:, :], far_w[:, :], float(-P), op=ALU.add).then_inc(fb_added, 1)
                            dve.wait_ge(fb_summed, at)
                            window = bass.ds(w * P, P)
                            nc.vector.tensor_tensor(agg[:, window], agg[:, window], sum_ps[0], ALU.add).then_inc(fb_added, 1)
                            if layer == 0:
                                nc.vector.tensor_tensor(cnt[:, window], cnt[:, window], cnt_ps[0], ALU.add)\
                                    .then_inc(fb_added, 1)
                            else:
                                dve.engine_nop().then_inc(fb_added, 1)
                        nc.vector.tensor_copy(far_w[:, :], far[:, bass.ds(g * C, C)]).then_inc(fb_added, 1)
                        loop(dve, WINDOWS, fb_window)
                    loop(dve, GROUPS, fb_group)

                if layer == 0:
                    steps.done(nc.vector.tensor_single_scalar(rinv[:, :], cnt[:, :], 1.0, op=ALU.max))
                    steps.wait()
                    steps.done(nc.vector.reciprocal(rinv[:, :], rinv[:, :]))
                    steps.wait()

                if layer == 2:
                    for h in range(2):
                        dve.wait_ge(h_copied[h], STEPS)
                def post(i, first):
                    for h, (_, n) in enumerate(HALVES):
                        if layer == 2 and first:
                            dve.wait_ge(y_done[h], STEPS)
                        elif layer > 0 or not first:
                            dve.wait_ge(post_done[h], i + layer * STEPS)
                        nc.vector.tensor_tensor(mean_T[h][:, :], agg[:, nodes(i, h)], rinv[:, nodes(i, h)], ALU.mult)\
                            .then_inc(mean_ready[h], 1)
                        if layer < 2:
                            nc.vector.tensor_single_scalar(has_in[h][0:1, :], cnt[0:1, nodes(i, h)], 1.0, op=ALU.min)\
                                .then_inc(mean_ready[h], 1)
                    if layer > 0:
                        to = xres if layer == 1 else hres
                        for h, (_, n) in enumerate(HALVES):
                            dve.wait_ge(post_done[h], i + (layer * STEPS + 1))
                            nc.vector.tensor_tensor(to[:, tiles(i, h), :], post_ps[h][:, 0:n, :], to[:, tiles(i, h), :],
                                                    ALU.add).then_inc(post_read[h], 1)
                            dve.wait_ge(post_read[h], i + ((layer - 1) * STEPS + 1))
                            steps.done(tile_stats(to, i, h))
                if layer == 0:
                    loop(dve, STEPS, post, peel=True)
                    continue
                steps.loop(STEPS, 2, post, peel=True)
                mean_and_var()
                make_norm(layer + 1)

                if layer == 1:
                    def transposed(i, first):
                        for h, (_, n) in enumerate(HALVES):
                            dve.wait_ge(tr_done[h], i + 1)
                            if not first:
                                dve.wait_ge(y_done[h], i)
                            nc.vector.tensor_copy(mean_T[h][:, :], tr_ps[h][:, 0:n * P]).then_inc(tr_read[h], 1)
                    loop(dve, STEPS, transposed, peel=True)
                    for h in range(2):
                        dve.wait_ge(h_ready[h], STEPS)
                    nc.vector.tensor_tensor(xres[:, :, :], xres[:, :, :],
                                            b_all[:, :].unsqueeze(1).broadcast_to([P, TILES, F]), ALU.add)
                else:
                    def scale(i, first):
                        for h, (_, n) in enumerate(HALVES):
                            dve.wait_ge(h_ready[h], i + (STEPS + 1))
                            dve.wait_ge(stored[h], i * 16 + 16 * STEPS * LAYERS)
                            nc.vector.tensor_tensor(oslot[h][:, :, :], hslot[h][:, :, :],
                                                    g_all[:, :].unsqueeze(1).broadcast_to([P, n, F]), ALU.mult)\
                                .then_inc(scaled[h], 1)
                    loop(dve, STEPS, scale)


def kernel(**inputs):
    import numpy as np
    import concourse.bacc as bacc
    from concourse import mybir
    from concourse.bass_utils import run_bass_kernel_spmd

    a = {k: np.ascontiguousarray(v) for k, v in inputs.items()}
    N, F = a["x"].shape
    E = a["src"].shape[0]
    GE = 8 * P
    groups = -(-E // GE)
    groups += groups % 2
    rows = -(-N // P) * P
    types = a["L1_gnn_edge_emb_W"].shape[0]

    def padded(e, fill):
        return np.concatenate([e.astype(np.int32), np.full(groups * GE - E, fill, np.int32)])

    def by_partition(e):
        return np.ascontiguousarray(e.reshape(groups * 8, P).T)

    dst = padded(a["dst"], N)
    etype = padded(a["edge_type_16"], 0).reshape(groups, 1, GE)
    arrays = {
        "x": np.concatenate([a["x"], np.zeros((rows - N, F), a["x"].dtype)]),
        "src": by_partition(padded(a["src"], 0)),
        "dst": by_partition(dst),
        "first_dst": np.ascontiguousarray(dst[::GE]),
        "etype": np.ascontiguousarray(np.broadcast_to(etype, (groups, types, GE))),
        "W1T": a["L0_gnn_W1"].T, "b1": a["L0_gnn_b1"], "W2T": a["L0_gnn_W2"].T, "b2": a["L0_gnn_b2"],
        "embT": a["L1_gnn_edge_emb_W"].T, "msgWT": a["L1_gnn_msg_W"].T, "msg_b": a["L1_gnn_msg_b"],
        "updWT": a["L1_gnn_upd_W"].T, "upd_b": a["L1_gnn_upd_b"], "ln_g": a["L1_gnn_ln_g"], "ln_b": a["L1_gnn_ln_b"],
    }
    arrays = {k: np.ascontiguousarray(v) for k, v in arrays.items()}
    nc = bacc.Bacc("TRN2", target_bir_lowering=False, num_devices=1)
    args = {k: nc.dram_tensor(f"in_{k}", v.shape, mybir.dt.from_np(v.dtype), kind="ExternalInput").ap()
            for k, v in arrays.items()}
    out = nc.dram_tensor("out_dram", (rows, F), mybir.dt.float32, kind="ExternalOutput").ap()
    gnn_program(nc, N, E, groups, **args, out=out)
    r = run_bass_kernel_spmd(nc, [{f"in_{k}": v for k, v in arrays.items()}], core_ids=[0])
    return r.results[0]["out_dram"][:N]
```

```python
import concourse.bass as bass
from concourse import mybir
from contextlib import ExitStack

P = 128
C = 8
GE = C * P
GROUPS_STEP = 4
STEPS_MAIN = 13
BLOCK_C = GROUPS_STEP * C
GROUPS = 2 * STEPS_MAIN * GROUPS_STEP


def gnn_program(nc, N, x, src, dst, first_dst, etype_cols, etype, W1T, b1, W2T, b2, embT, msgWT, msg_b,
                updWT, upd_b, ln_g, ln_b, out):
    fp32 = mybir.dt.float32
    fp16 = mybir.dt.float16
    bf16 = mybir.dt.bfloat16
    i32 = mybir.dt.int32
    ALU = mybir.AluOpType
    ACT = mybir.ActivationFunctionType
    AX = mybir.AxisListType

    F = x.shape[1]
    TILES = x.shape[0] // P
    SPILL = 3
    BUCKETS = TILES + SPILL
    ETD, TYPES = embT.shape
    LAYERS = 3
    B = STEPS_MAIN
    FIRST_GROUP = B * GROUPS_STEP
    BLOCK_COLS = (B + 1) * BLOCK_C
    WIN_G, WIN_B = P, 2 * P
    WINDOWS = TILES + 1
    COLS = WINDOWS * P + P
    UNITS = []
    while sum(map(len, UNITS)) < BUCKETS:
        at = sum(map(len, UNITS))
        UNITS.append(range(at, at + (7 if len(UNITS) < 4 else 6)))
    U, J = len(UNITS), 7
    R = 13
    assert sum(map(len, UNITS)) == BUCKETS == 4 * R and U % 2 == 0
    assert N + WIN_G <= COLS and N - 1 + WIN_B <= COLS
    HALVES = ((0, 4), (4, 3))
    STEP = 7
    STEPS = TILES // STEP
    EPS = 1e-5
    K3 = 3

    ctx = ExitStack()
    with ctx:
        def sb(name, shape, dt=fp32):
            return ctx.enter_context(nc.sbuf_tensor(name, shape, dt))

        def sem(name):
            return ctx.enter_context(nc.semaphore(name))

        def sems(name, n):
            return [sem(f"{name}{k}") for k in range(n)]

        tab = [nc.dram_tensor(f"table{k}", (TILES * P, F if k == 2 else K3 * F), fp32 if k == 2 else bf16,
                              kind="Internal").ap() for k in range(LAYERS)]
        tab_v = [t.rearrange("(t p) f -> p t f", p=P) for t in tab]
        src_tab = nc.dram_tensor("src_tab", (B + 1, BUCKETS, P), bf16, kind="Internal").ap()
        type_tab = nc.dram_tensor("type_tab", (B + 1, BUCKETS, P), bf16, kind="Internal").ap()
        rinv_tab = nc.dram_tensor("rinv_tab", (1, TILES * P), fp32, kind="Internal").ap()
        x_v = x.rearrange("(t p) f -> p t f", p=P)
        out_v = out.rearrange("(t p) f -> p t f", p=P)

        src_all = sb("src_all", [P, (GROUPS + 2) * C], i32)
        dst_all = sb("dst_all", [P, GROUPS * C], i32)
        base_all = sb("base_all", [P, GROUPS], i32)
        rel = sb("rel", [P, GROUPS * C])
        far = sb("far", [P, GROUPS * C])
        tile_no = sb("tile_no", [P, BLOCK_COLS], fp16)
        codes = sb("codes", [P, 2, BLOCK_COLS], fp16)
        first_tile = sb("first_tile", [P, GROUPS], i32)
        rank1 = sb("rank1", [P, BLOCK_COLS])
        slot_dst = sb("slot_dst", [P, (B + 1) * BUCKETS])
        far_max = sb("far_max", [P, 1])
        far_one = sb("far_one", [P, 1])
        flag = sb("flag", [1, 1], i32)
        far_w = sb("far_w", [P, C])
        fb_idx_cols = sb("fb_idx_cols", [P, C], i32)
        columns = sb("columns", [P, P])
        columns_b = sb("columns_b", [P, P], bf16)
        columns1_b = sb("columns1_b", [P, WIN_B], bf16)
        columns1 = sb("columns1", [P, WIN_B])
        columns1_h = sb("columns1_h", [P, P], fp16)
        part_no = sb("part_no", [P, 1])
        part_i = sb("part_i", [K3 * TYPES, 2], i32)
        type_no = sb("type_no", [K3 * TYPES, 1])
        third = sb("third", [K3 * TYPES, 1])
        masks = sb("masks", [K3 * TYPES, K3])
        ones = sb("ones", [P, P])
        ones_b = sb("ones_b", [P, P], bf16)
        ident = sb("ident", [P, P])
        below = sb("below", [P, P], fp16)
        eps = sb("eps", [P, 1])
        w1 = sb("w1", [P, F])
        w2 = sb("w2", [P, F])
        wm = sb("wm", [P, F])
        wt = sb("wt", [ETD, F])
        wu = sb("wu", [P, F])
        emb = sb("emb", [ETD, K3, TYPES])
        rows_b = sb("rows_b", [1, 4, F])
        g_all = sb("g_all", [P, F])
        b_all = sb("b_all", [P, F])
        type_f = sb("type_f", [K3 * TYPES, 2, F])
        type_p = sb("type_p", [K3 * TYPES, K3, F], bf16)
        type_rows = sb("type_rows", [K3 * TYPES, F], bf16)
        idx = [sb(f"idx{s}", [P, C], i32) for s in range(2)]
        rows = [sb(f"rows{s}", [P, C, K3 * F], bf16) for s in range(2)]
        rows_f = [r[:, :, :].rearrange("p c f -> p (c f)")[:, 0:2 * GE].bitcast(fp32).rearrange("p (c f) -> p c f", f=F)
                  for r in rows]
        hot = [sb(f"hot{s}", [P, C, P]) for s in range(2)]
        hot_b = [h[:, :, :].rearrange("p c f -> p (c f)").bitcast(bf16)[:, 0:GE].rearrange("p (c f) -> p c f", f=P)
                 for h in hot]
        src_in = [sb(f"src_in{s}", [P, J * P], bf16) for s in range(2)]
        src_hot = [sb(f"src_hot{s}", [P, J * P], bf16) for s in range(2)]
        agg = sb("agg", [P, COLS])
        x_or_cnt = sb("x_or_cnt", [P, COLS])
        cnt = x_or_cnt[:, :]
        xres = x_or_cnt[:, 0:TILES * F].rearrange("p (t f) -> p t f", f=F)
        htab = sb("htab", [P, TILES, K3 * F], bf16)
        stats = sb("stats", [P, TILES, 6])
        mean = sb("mean", [P, TILES])
        var = sb("var", [P, TILES])
        std = sb("std", [P, TILES])
        rstd = [sb(f"rstd{k}", [P, TILES]) for k in range(3)]
        nmr = [sb(f"nmr{k}", [P, TILES]) for k in range(3)]

        def carve(region, at, shape, dt, size):
            n = 1
            for d in shape[1:]:
                n *= d
            a = region[0:shape[0], at // 4:(at + n * size + 3) // 4]
            a = a if dt == fp32 else a.bitcast(dt)[:, 0:n]
            if len(shape) == 3:
                a = a.rearrange("p (a b) -> p a b", b=shape[2])
            return a, at + (n * size + 3) // 4 * 4

        def carver(region):
            at = [0]

            def take(shape, dt=fp32, size=4):
                a, at[0] = carve(region, at[0], shape, dt, size)
                return a
            return take

        region_a = sb("region_a", [P, 6300])
        take = carver(region_a)
        dst_hot = [take([P, J, WIN_B], bf16, 2) for _ in range(2)]
        picked = [take([P, J, K3 * F], bf16, 2) for _ in range(2)]
        take = carver(region_a)
        dst_hot_f = [take([P, J, WIN_B]) for _ in range(2)]
        messages = [take([P, J, F]) for _ in range(2)]
        take = carver(region_a)
        mean_T = [take([P, n * P]) for _, n in HALVES]
        hslot = [take([P, n, F]) for _, n in HALVES]
        rslot = [take([P, n, F]) for _, n in HALVES]
        oslot = [take([P, n, F]) for _, n in HALVES]
        has_in = [take([1, n * P]) for _, n in HALVES]
        rinv = [take([P, n * P]) for _, n in HALVES]
        region_b = sb("region_b", [P, 7500])
        take = carver(region_b)
        BC, T = BLOCK_C, TILES
        in_tile = take([P, T, BC], fp16, 2)
        seen = take([P, T, BC], fp16, 2)
        prod = take([P, T, BC], fp16, 2)
        scan_mask = take([P, T, BC], fp16, 2)
        coded = take([P, 2 * BUCKETS, BC], fp16, 2)
        slot_hot = take([P, BC, P], fp16, 2)
        code_i = take([P, 3 * BUCKETS], i32)
        code_f = take([P, 2, BUCKETS])
        code_T = take([BUCKETS, 2 * P], bf16, 2)
        sort_small = take([P, 4, BC])
        split_codes = [take([P, 2, BC], fp16, 2) for _ in range(2)]
        take = carver(region_b)
        types_in = [take([K3 * TYPES, GE], i32) for _ in range(2)]
        types_hot = [take([K3 * TYPES, GE], bf16, 2) for _ in range(2)]
        btypes_in = [take([K3 * TYPES, J * P], bf16, 2) for _ in range(2)]
        btypes_hot = [take([K3 * TYPES, J * P], bf16, 2) for _ in range(2)]
        tile_cols = sb("tile_cols", [P, T], fp16)

        banks = ctx.enter_context(nc.psum_tensor("banks", [P, 8, 512], fp32))
        sum_ps = [banks[:, 0, 2 * s * P:(2 * s + 1) * P] for s in range(2)]
        cnt_ps = [banks[:, 0, (2 * s + 1) * P:(2 * s + 2) * P] for s in range(2)]
        bsum_ps = banks[:, 1, 0:WIN_B]
        bcnt_ps = banks[:, 2, 0:WIN_B]
        before_ps = banks[:, 3, 0:T]
        table_ps = banks[:, 3, 64:64 + 2 * BUCKETS]
        code_T_ps = banks[0:BUCKETS, 3, 256:512]
        pick_ps = [banks[:, 4 + k, 0:K3 * F] for k in range(4)]
        type_ps = banks[:, 2:4, :].rearrange("p b (c f) -> p (b c) f", f=F)
        message_ps = [banks[:, 4 + 2 * s:6 + 2 * s, :].rearrange("p b (t f) -> p (b t) f", f=F) for s in range(2)]
        post_ps = [banks[:, 4 + h, :].rearrange("p (t f) -> p t f", f=F) for h in range(2)]
        tr_ps = [banks[:, 6 + h, :] for h in range(2)]
        setup_ps = banks[:, 7, :]

        edges_in = sem("edges_in")
        x_in = sem("x_in")
        weights_in = sem("weights_in")
        consts = sem("consts")
        cleared = sem("cleared")
        dve_step = sem("dve_step")
        far_ready = sem("far_ready")
        far_known = sem("far_known")
        setup_done = sem("setup_done")
        type_rows_ready = sem("type_rows_ready")
        idx_ready = sems("idx_ready", 4)
        gathered = sems("gathered", 4)
        hot_ready = sems("hot_ready", 4)
        summed = sems("summed", 4)
        types_loaded = sems("types_loaded", 4)
        types_hot_ready = sems("types_hot_ready", 4)
        types_done = sems("types_done", 4)
        pre_ready = sems("pre_ready", 4)
        msgs_ready = sems("msgs_ready", 4)
        added = sems("added", 5)
        counted = sems("counted", 5)
        src_loaded = sems("src_loaded", U)
        src_hot_ready = sem("src_hot_ready")
        dst_hot_ready = sem("dst_hot_ready")
        unit_picked = sem("unit_picked")
        unit_summed = sem("unit_summed")
        pick_done = sems("pick_done", R)
        pick_read = sems("pick_read", R)
        messages_ready = sem("messages_ready")
        in_tile_ready = sem("in_tile_ready")
        before_done = sem("before_done")
        coded_ready = sem("coded_ready")
        table_done = sem("table_done")
        code_f_ready = sem("code_f_ready")
        code_T_done = sem("code_T_done")
        code_T_ready = sem("code_T_ready")
        code_T_stored = sem("code_T_stored")
        fb_idx = sem("fb_idx")
        fb_gathered = sem("fb_gathered")
        fb_types_in = sem("fb_types_in")
        fb_types_hot = sem("fb_types_hot")
        fb_types_done = sem("fb_types_done")
        fb_pre = sem("fb_pre")
        fb_msgs = sem("fb_msgs")
        fb_hot = sem("fb_hot")
        fb_summed = sem("fb_summed")
        fb_added = sem("fb_added")
        rinv_ready = sems("rinv_ready", 2)
        rinv_stored = sems("rinv_stored", 2)
        rinv_loaded = sems("rinv_loaded", 2)
        mean_ready = sems("mean_ready", 2)
        post_done = sems("post_done", 2)
        post_read = sems("post_read", 2)
        stats_ready = sem("stats_ready")
        std_ready = sem("std_ready")
        norm_ready = sem("norm_ready")
        h_ready = sems("h_ready", 2)
        rest_h = sems("rest_h", 2)
        second_h = sems("second_h", 2)
        parts_ready = sems("parts_ready", 2)
        tr_done = sems("tr_done", 2)
        tr_read = sems("tr_read", 2)
        y_done = sems("y_done", 2)
        z_ready = sems("z_ready", 2)
        scaled = sems("scaled", 2)
        out_ready = sems("out_ready", 2)
        stored = sems("stored", 2)
        out_stored = sems("out_stored", 2)

        EDGE_LOADS = 5 * 16
        WEIGHT_LOADS = 14 * 16
        CONSTS = 13
        FB_ALL = GROUPS * WINDOWS

        block = ctx.enter_context(nc.Block())

        def loop(eng, n, step, peel=False):
            if peel:
                step(0, True)
            with eng.Fori(1 if peel else 0, n) as i:
                step(i, False)

        class Steps:

            def __init__(self, eng):
                self.eng, self.base, self.n = eng, 0, 0

            def done(self, ins):
                ins.then_inc(dve_step, 1)
                self.n += 1

            def wait(self):
                self.eng.wait_ge(dve_step, self.base + self.n)

            def loop(self, n, per, step, peel=False):
                start = self.base + self.n

                def one(i, first):
                    self.base, self.n = i * per + start, 0
                    step(i, first)
                    assert self.n == per, self.n
                loop(self.eng, n, one, peel)
                self.base, self.n = start + n * per, 0

        class Count:

            def __init__(self, eng, layer, b, first, own=()):
                self.eng, self.layer, self.b, self.first = eng, layer, b, first
                self.K = b + layer * B
                self.have = {}
                self.none = first and layer == 0
                if not first:
                    for times, plus in [(1, 0), (1, 1)] + [(U, k) for k in range(-1, U + 1)] + list(own):
                        self(times, plus)

            def __call__(self, times, plus):
                if self.first:
                    return times * self.K + plus
                if (times, plus) not in self.have:
                    self.have[times, plus] = self.eng.snap(self.eng.to_reg(self.K * times + plus))
                return self.have[times, plus]

            def unit(self, u, last_step=False, since=0):
                return self(U, u + 1 - (U if last_step else 0) - since * B * U)

            def bucket(self, t):
                return self(BUCKETS // R, t // R + 1)

            def here(self, times=1):
                return self(times, times)

            def before(self, times=1):
                return self(times, 0)

        def tiles(i, h):
            t0, n = HALVES[h]
            return bass.ds(i * STEP + t0, n)

        def nodes(i, h):
            t0, n = HALVES[h]
            return bass.ds(i * (STEP * P) + t0 * P, n * P)

        part = lambda k: slice(k * F, (k + 1) * F)
        GROUP_AFTER = (1, 3, 5, 7)
        GROUP_TYPES = (0, 2, 4, 6)
        SORT_N = lambda c: c(1, 2)
        hres = htab[:, :, 0:2 * F].bitcast(fp32)


        @block.sync
        def _(sp):
            sp.dma_start(src_all[:, 0:GROUPS * C], src).then_inc(edges_in, 16)
            sp.dma_start(src_all[:, GROUPS * C:], src[:, FIRST_GROUP * C:(FIRST_GROUP + 2) * C]).then_inc(edges_in, 16)
            sp.dma_start(dst_all[:, :], dst).then_inc(edges_in, 16)
            sp.dma_start(base_all[:, :], first_dst.partition_broadcast(P)).then_inc(edges_in, 16)
            sp.dma_start(far[:, 0:BLOCK_COLS].bitcast(i32), etype_cols[:, 0:BLOCK_COLS]).then_inc(edges_in, 16)
            sp.dma_start(xres, x_v).then_inc(x_in, 16)
            for to, w in ((w1, W1T), (w2, W2T), (wm, msgWT[0:F, :]), (wt, msgWT[F:F + ETD, :]), (wu, updWT)):
                sp.dma_start(to[:, :], w).then_inc(weights_in, 16)
            for k in range(K3):
                sp.dma_start(emb[:, k, :], embT).then_inc(weights_in, 16)
            for k, b in enumerate((b1, b2, msg_b, upd_b)):
                sp.dma_start(rows_b[0:1, k, :], b.rearrange("(a f) -> a f", a=1)).then_inc(weights_in, 16)
            sp.dma_start(g_all[:, :], ln_g.partition_broadcast(P)).then_inc(weights_in, 16)
            sp.dma_start(b_all[:, :], ln_b.partition_broadcast(P)).then_inc(weights_in, 16)

            def store_codes(b, n):
                sp.wait_ge(code_T_ready, n)
                for k, to in enumerate((src_tab, type_tab)):
                    sp.dma_start(to[bass.ds(b, 1), :, :].rearrange("a t s -> (a t) s"), code_T[:, k * P:(k + 1) * P])\
                        .then_inc(code_T_stored, 16)

            def load_types(to, g, done):
                sp.dma_start(to, etype[bass.ds(g, 1), :, :].rearrange("a r e -> (a r) e")).then_inc(done, 16)

            def store_table(layer):
                def step(i, first):
                    for h in range(2):
                        if layer == 1:
                            sp.wait_ge(rinv_ready[h], i + 1)
                            sp.dma_start(rinv_tab[:, nodes(i, h)], rinv[h][0:1, :]).then_inc(rinv_stored[h], 16)
                    for h, (_, n) in enumerate(HALVES):
                        sp.wait_ge(parts_ready[h], i + (layer * STEPS + 1))
                        sp.dma_start(tab_v[layer][:, tiles(i, h), :], oslot[h] if layer == 2 else htab[:, tiles(i, h), :])\
                            .then_inc(stored[h], 16)
                loop(sp, STEPS, step)

            def load_rinv(layer):
                for h in range(2):
                    sp.wait_ge(rinv_stored[h], 16 * STEPS)
                sp.wait_ge(added[4], (layer + 1) * B)

                def step(i, first):
                    for h, (_, n) in enumerate(HALVES):
                        if not first:
                            sp.wait_ge(mean_ready[h], i * 2 + 2 * STEPS if layer == 1 else i + 4 * STEPS)
                        sp.dma_start(rinv[h], rinv_tab[:, nodes(i, h)].broadcast_to([P, n * P])).then_inc(rinv_loaded[h], 16)
                loop(sp, STEPS, step, peel=True)

            store_codes(0, 1)
            for layer in range(LAYERS):
                if layer == 2:
                    load_rinv(1)
                store_table(layer)
                if layer == 1:
                    for h in range(2):
                        sp.wait_ge(rinv_ready[h], STEPS)
                    sp.dma_start(xres, x_v).then_inc(x_in, 16)

                def step(b, first):
                    c = Count(sp, layer, b, first, [(32, 32)] if layer == 0 else [])
                    for u in range(U):
                        if layer == 0:
                            sp.wait_ge(code_T_stored, c(32, 32))
                        if not (c.none and u < 2):
                            sp.wait_ge(src_hot_ready, c.unit(u - 2))
                        slots = len(UNITS[u]) * P
                        flat = lambda t: t[bass.ds(b, 1), UNITS[u][0]:UNITS[u][-1] + 1, :].rearrange("a t s -> a (t s)")\
                            .broadcast_to
                        sp.dma_start(src_in[u % 2][:, 0:slots], flat(src_tab)([P, slots])).then_inc(src_loaded[u], 16)
                        if layer == 2:
                            sp.dma_start(btypes_in[u % 2][:, 0:slots], flat(type_tab)([K3 * TYPES, slots]))\
                                .then_inc(src_loaded[u], 16)
                        if layer == 2 and u % 2 == 0:
                            gi = u // 2
                            if gi > 1 or not first:
                                sp.wait_ge(types_hot_ready[(gi + 2) % 4], b if gi < 2 else b + 1)
                            load_types(types_in[gi % 2], b * GROUPS_STEP + (FIRST_GROUP + gi), types_loaded[gi])
                        if layer == 0 and u == 5:
                            store_codes(b + 1, b + 2)
                loop(sp, B, step, peel=layer != 1)

            sp.wait_ge(far_known, 1)
            with sp.If(sp.value_load(flag[0:1, 0:1], min_val=0, max_val=P) > 0):
                sp.wait_ge(added[4], LAYERS * B)
                def fb_step(g, first):
                    if not first:
                        sp.wait_ge(fb_types_hot, g)
                    load_types(types_in[0], g, fb_types_in)
                loop(sp, GROUPS, fb_step, peel=True)

            load_rinv(2)

            def store_out(i, first):
                for h in range(2):
                    sp.wait_ge(out_ready[h], i + 1)
                    sp.dma_start(out_v[:, tiles(i, h), :], oslot[h]).then_inc(out_stored[h], 16)
            loop(sp, STEPS, store_out)
            for h in range(2):
                sp.wait_ge(out_stored[h], 16 * STEPS)
            sp.wait_ge(code_T_stored, 32 * (B + 1))

        @block.gpsimd
        def _(pool):
            def iota(to, pattern, base, mult):
                nc.gpsimd.iota(to, pattern, base=base, channel_multiplier=mult,
                               allow_small_or_imprecise_dtypes=True).then_inc(consts, 1)
            iota(columns[:, :], [[1, P]], 0, 0)
            iota(columns_b[:, :], [[1, P]], 0, 0)
            iota(columns1_b[:, :], [[1, WIN_B]], 1, 0)
            iota(columns1[:, :], [[1, WIN_B]], 1, 0)
            iota(columns1_h[:, :], [[1, P]], 1, 0)
            iota(tile_cols[:, :], [[1, T]], 0, 0)
            iota(part_no[:, :], [[0, 1]], 0, 1)
            iota(part_i[:, 0:1], [[0, 1]], 0, 1)
            nc.gpsimd.memset(ones_b[:, :], 1.0).then_inc(consts, 1)
            nc.gpsimd.memset(eps[:, :], EPS).then_inc(consts, 1)
            nc.gpsimd.memset(ones[:, :], 1.0).then_inc(consts, 1)
            nc.gpsimd.memset(below[:, :], 1.0).then_inc(cleared, 1)
            nc.gpsimd.memset(ident[:, :], 0.0).then_inc(cleared, 1)
            pool.wait_ge(cleared, 2)
            nc.gpsimd.affine_select(out=ident[:, :], in_=ident[:, :], compare_op=ALU.not_equal, fill=1.0,
                                    base=0, pattern=[[-1, P]], channel_multiplier=1).then_inc(consts, 1)
            nc.gpsimd.affine_select(out=below[:, :], in_=below[:, :], compare_op=ALU.is_gt, fill=0.0,
                                    base=0, pattern=[[1, P]], channel_multiplier=-1).then_inc(consts, 1)

            def second_parts(layer):
                def step(i, first):
                    for h in range(2):
                        pool.wait_ge(rest_h[h], i + (layer * STEPS + 1))
                        nc.gpsimd.tensor_copy(htab[:, tiles(i, h), part(1)], rslot[h]).then_inc(second_h[h], 1)
                loop(pool, STEPS, step)

            def table_complete(layer):
                for h in range(2):
                    pool.wait_ge(stored[h], 16 * STEPS * (layer + 1))

            def gather(layer, to, cols, done):
                for c in range(C):
                    nc.gpsimd.indirect_dma_start(
                        out=to[:, c, :], out_offset=None, in_=tab[layer],
                        in_offset=bass.IndirectOffsetOnAxis(ap=cols[:, c:c + 1], axis=0)).then_inc(done, 16)

            second_parts(0)
            for layer in range(LAYERS):
                to = rows_f if layer == 2 else rows

                def step(b, first):
                    c = Count(pool, layer, b, first)
                    for gi in range(GROUPS_STEP):
                        table_complete(layer)
                        pool.wait_ge(idx_ready[gi], c.here())
                        if not (c.none and gi < 2):
                            pool.wait_ge(summed[(gi + 2) % 4], c.before() if gi < 2 else c.here())
                        gather(layer, to[gi % 2], idx[gi % 2], gathered[gi])
                loop(pool, B, step, peel=layer == 0)

                if layer == 0:
                    pool.wait_ge(far_known, 1)
                    far_n = pool.value_load(flag[0:1, 0:1], min_val=0, max_val=P)
                with pool.If(far_n > 0):
                    def fb_step(g, first):
                        g1 = pool.snap(pool.to_reg(g + (layer * GROUPS + 1)))
                        table_complete(layer)
                        pool.wait_ge(fb_idx, g1)
                        gather(layer, to[0], fb_idx_cols, fb_gathered)
                    loop(pool, GROUPS, fb_step)
                if layer < 2:
                    second_parts(layer + 1)

            def residual(i, first):
                for h in range(2):
                    pool.wait_ge(scaled[h], i + 1)
                    nc.gpsimd.tensor_tensor(oslot[h], oslot[h], xres[:, tiles(i, h), :], ALU.add).then_inc(out_ready[h], 1)
            loop(pool, STEPS, residual)

        @block.scalar
        def _(act):
            def normalise(i, h, to, func, inp, k):
                t0, n = HALVES[h]
                for j in range(n):
                    t = bass.ds(i * STEP + (t0 + j), 1)
                    last = nc.scalar.activation(to[h][:, j:j + 1, :], inp(j, t), func,
                                                bias=nmr[k][:, t], scale=rstd[k][:, t])
                return last

            def make_std(k):
                act.wait_ge(stats_ready, k)
                nc.scalar.activation(std[:, :], var[:, :], ACT.Sqrt, bias=eps[:, 0:1]).then_inc(std_ready, 1)
                act.wait_ge(norm_ready, k)

            def first_parts(i, h, layer, what, value):
                what.then_inc(h_ready[h], 1)
                act.wait_ge(h_ready[h], i * 2 + (layer * 2 * STEPS + 1))
                nc.scalar.activation(htab[:, tiles(i, h), part(0)], value[h], ACT.Copy).then_inc(h_ready[h], 1)

            x_tiles = lambda j, t: xres[:, t, :]

            act.wait_ge(consts, CONSTS)
            make_std(1)

            def first_rows(i, first):
                for h in range(2):
                    if not first:
                        act.wait_ge(rest_h[h], i)
                    first_parts(i, h, 0, normalise(i, h, hslot, ACT.Relu, x_tiles, 0), hslot)
            loop(act, STEPS, first_rows, peel=True)

            for layer in range(LAYERS):
                def step(b, first):
                    c = Count(act, layer, b, first, [(U, k - 2 * B * U) for k in range(-1, U + 1)] if layer == 2
                              else [(BUCKETS // R, k) for k in range(BUCKETS // R + 1)])
                    for u in range(U):
                        if layer < 2:
                            for j, t in enumerate(UNITS[u]):
                                act.wait_ge(pick_done[t % R], c.bucket(t))
                                nc.scalar.activation(picked[u % 2][:, j, :], pick_ps[t % 4], ACT.Copy)\
                                    .then_inc(pick_read[t % R], 1)
                            continue
                        act.wait_ge(unit_picked, c.unit(u, since=2))
                        if not (first and u < 2):
                            act.wait_ge(unit_summed, c.unit(u - 2))
                        m = len(UNITS[u])
                        nc.scalar.activation(messages[u % 2][:, 0:m, :], message_ps[u % 2][:, 0:m, :], ACT.Relu)\
                            .then_inc(messages_ready, 1)
                        if u in GROUP_TYPES:
                            gi = GROUP_TYPES.index(u)
                            act.wait_ge(pre_ready[gi], b + 1)
                            nc.scalar.activation(rows_f[gi % 2], rows_f[gi % 2], ACT.Relu).then_inc(msgs_ready[gi], 1)
                loop(act, B, step, peel=layer != 1)

                if layer == 2:
                    act.wait_ge(far_known, 1)
                    with act.If(act.value_load(flag[0:1, 0:1], min_val=0, max_val=P) > 0):
                        def fb_step(g, first):
                            act.wait_ge(fb_pre, g + 1)
                            nc.scalar.activation(rows_f[0], rows_f[0], ACT.Relu).then_inc(fb_msgs, 1)
                        loop(act, GROUPS, fb_step)

                def layer0_rows(i, first):
                    for h in range(2):
                        act.wait_ge(post_done[h], i + 1)
                        act.wait_ge(rest_h[h], i + STEPS)
                        first_parts(i, h, 1, nc.scalar.activation(hslot[h], post_ps[h][:, 0:HALVES[h][1], :], ACT.Relu),
                                    hslot)

                def layer1_rows(i, first):
                    for h in range(2):
                        if not first:
                            act.wait_ge(tr_done[h], i)
                        normalise(i, h, hslot, ACT.Relu, x_tiles, 1).then_inc(z_ready[h], 1)
                    for h in range(2):
                        act.wait_ge(y_done[h], i + 1)
                        if not first:
                            act.wait_ge(rest_h[h], i + 2 * STEPS)
                            act.wait_ge(stored[h], i * 16 + 16 * 2 * STEPS)
                        first_parts(i, h, 2, nc.scalar.activation(oslot[h], post_ps[h][:, 0:HALVES[h][1], :], ACT.Copy),
                                    oslot)
                if layer == 0:
                    loop(act, STEPS, layer0_rows)
                elif layer == 1:
                    make_std(2)
                    loop(act, STEPS, layer1_rows, peel=True)

            act.wait_ge(added[4], LAYERS * B)
            def input_again(i, first):
                for h in range(2):
                    if not first:
                        act.wait_ge(post_read[h], i + STEPS)
                    normalise(i, h, hslot, ACT.Relu, x_tiles, 1).then_inc(h_ready[h], 1)
            loop(act, STEPS, input_again, peel=True)
            make_std(3)

            def last_rows(i, first):
                for h in range(2):
                    if not first:
                        act.wait_ge(scaled[h], i)
                    normalise(i, h, rslot, ACT.Identity, lambda j, t: hres[:, t, :], 2).then_inc(z_ready[h], 1)
            loop(act, STEPS, last_rows, peel=True)

        @block.tensor
        def _(pe):
            def mm(to, left, right, start=True, stop=True):
                return nc.tensor.matmul(to, left, right, start=start, stop=stop)

            pe.wait_ge(weights_in, WEIGHT_LOADS)
            pe.wait_ge(consts, CONSTS)
            mm(setup_ps[0:K3 * TYPES, 0:F], emb[:, :, :].rearrange("e k t -> e (k t)"), wt[:, :]).then_inc(setup_done, 1)

            def window_sum(layer, s):
                for c in range(C):
                    if layer == 2:
                        last = mm(sum_ps[s], rows_f[s][:, c, :], hot[s][:, c, :], c == 0, c == C - 1)
                        continue
                    for k in range(K3):
                        last = mm(sum_ps[s], rows[s][:, c, part(k)], hot_b[s][:, c, :],
                                  (c, k) == (0, 0), (c, k) == (C - 1, K3 - 1))
                return last

            def window_count(s):
                for c in range(C):
                    mm(cnt_ps[s], ones_b[:, :], hot_b[s][:, c, :], c == 0, c == C - 1)

            def type_rows_of_group(s):
                for c in range(C):
                    last = mm(type_ps[:, c, :], types_hot[s][:, c * P:(c + 1) * P], type_rows[:, :])
                return last

            def sort_before(n):
                pe.wait_ge(in_tile_ready, n)
                for c in range(BLOCK_C):
                    last = mm(before_ps, below[:, :], in_tile[:, :, c], c == 0, c == BLOCK_C - 1)
                last.then_inc(before_done, 1)

            def sort_table(n):
                pe.wait_ge(coded_ready, n)
                for c in range(BLOCK_C):
                    last = mm(table_ps, slot_hot[:, c, :], coded[:, :, c], c == 0, c == BLOCK_C - 1)
                last.then_inc(table_done, 1)

            def sort_turn(n, before):
                pe.wait_ge(consts, CONSTS)
                pe.wait_ge(code_f_ready, n)
                if before is not None:
                    pe.wait_ge(code_T_ready, before)
                for k in range(2):
                    last = nc.tensor.transpose(code_T_ps[:, k * P:(k + 1) * P], code_f[:, k, :], ident[:, :])
                last.then_inc(code_T_done, 1)

            def pick(layer, c, u, j):
                t, slots = UNITS[u][j], slice(j * P, (j + 1) * P)
                left = src_hot[u % 2][:, slots]
                tile = t if t < TILES else bass.ds(c.first_tile + (t - TILES), 1)
                if layer < 2:
                    return mm(pick_ps[t % 4], left, htab[:, tile, :])
                to = message_ps[u % 2][:, j, :]
                for k in range(K3):
                    mm(to, left, htab[:, tile, part(k)], k == 0, False)
                return mm(to, btypes_hot[u % 2][:, slots], type_rows[:, :], False, True)

            def slot_sum(layer, u, j):
                t = UNITS[u][j]
                begin, end = t == 0, t == BUCKETS - 1
                if layer == 2:
                    return mm(bsum_ps, messages[u % 2][:, j, :], dst_hot_f[u % 2][:, j, :], begin, end)
                right = dst_hot[u % 2][:, j, :]
                if layer == 0:
                    mm(bcnt_ps, ones_b[:, :], right, begin, end)
                for k in range(K3):
                    last = mm(bsum_ps, picked[u % 2][:, j, part(k)], right, begin and k == 0, end and k == K3 - 1)
                return last

            sort_before(1)
            sort_table(1)
            sort_turn(1, None)
            far_n = None
            for layer in range(LAYERS):
                def unit(c, u):
                    if u < U:
                        pe.wait_ge(src_hot_ready, c.unit(u))
                    if u > 0:
                        pe.wait_ge(dst_hot_ready, c.unit(u - 1))
                    if u == 1 and not c.none:
                        pe.wait_ge(added[4], c.before())
                    if layer == 2:
                        if u < U:
                            if not (c.first and u < 2):
                                pe.wait_ge(messages_ready, c.unit(u - 2, since=2))
                            for j in range(len(UNITS[u])):
                                last = pick(layer, c, u, j)
                            last.then_inc(unit_picked, 1)
                        if u > 0:
                            pe.wait_ge(messages_ready, c.unit(u - 1, since=2))
                            for j in range(len(UNITS[u - 1])):
                                last = slot_sum(layer, u - 1, j)
                            last.then_inc(unit_summed, 1)
                        return
                    for j in range(J):
                        if u < U and j < len(UNITS[u]):
                            t = UNITS[u][j]
                            if t >= 4 or not c.none:
                                pe.wait_ge(pick_read[(t - 4) % R], c.bucket(t - 4))
                            pick(layer, c, u, j).then_inc(pick_done[t % R], 1)
                        if u > 0 and j < len(UNITS[u - 1]):
                            t = UNITS[u - 1][j]
                            pe.wait_ge(pick_read[t % R], c.bucket(t))
                            last = slot_sum(layer, u - 1, j)
                    if u > 0:
                        last.then_inc(unit_summed, 1)

                def step(b, first):
                    c = Count(pe, layer, b, first, [
                        [(1, 2), (16 * C, 16 * C)] + [(BUCKETS // R, k) for k in range(BUCKETS // R + 1)],
                        [(16 * C, 16 * C)] + [(BUCKETS // R, k) for k in range(BUCKETS // R + 1)],
                        [(U, k - 2 * B * U) for k in range(-1, U + 1)]][layer])
                    c.first_tile = pe.value_load(first_tile[0:1, bass.ds(b * GROUPS_STEP, 1)], min_val=0,
                                                 max_val=TILES - SPILL)
                    for u in range(U):
                        gi = GROUP_AFTER.index(u) if u in GROUP_AFTER else None
                        if layer == 2 and u in GROUP_TYPES:
                            gt = GROUP_TYPES.index(u)
                            pe.wait_ge(types_hot_ready[gt], b + 1)
                            if gt > 0 or not first:
                                pe.wait_ge(pre_ready[(gt - 1) % 4], b if gt == 0 else b + 1)
                            type_rows_of_group(gt % 2).then_inc(types_done[gt], 1)
                        unit(c, u)
                        if layer == 0 and u == 1:
                            sort_before(SORT_N(c))
                        if layer == 0 and u == 3:
                            sort_table(SORT_N(c))
                        if layer == 0 and u == 4:
                            sort_turn(SORT_N(c), c(1, 1))
                        if gi is None:
                            continue
                        pe.wait_ge(hot_ready[gi], c.here())
                        if not (c.none and gi == 0):
                            seen_at = c.before() if gi == 0 else c.here()
                            pe.wait_ge(added[(gi + 3) % 4], seen_at)
                            if layer == 0:
                                pe.wait_ge(counted[(gi + 3) % 4], seen_at)
                        if layer == 0:
                            window_count(gi % 2)
                        if layer == 2:
                            pe.wait_ge(msgs_ready[gi], b + 1)
                        else:
                            pe.wait_ge(gathered[gi], c.here(16 * C))
                        window_sum(layer, gi % 2).then_inc(summed[gi], 1)
                    unit(c, U)
                if layer == 2:
                    pe.wait_ge(type_rows_ready, 1)
                for h in range(2):
                    pe.wait_ge(parts_ready[h], (layer + 1) * STEPS)
                loop(pe, B, step, peel=layer != 1)

                if layer == 0:
                    pe.wait_ge(far_ready, 1)
                    mm(setup_ps[0:1, F:F + 1], far_one[:, 0:1], ones[:, 0:1]).then_inc(setup_done, 1)
                    pe.wait_ge(far_known, 1)
                    far_n = pe.value_load(flag[0:1, 0:1], min_val=0, max_val=P)
                with pe.If(far_n > 0):
                    def fb_group(g, first):
                        if layer == 2:
                            pe.wait_ge(fb_types_hot, g + 1)
                            type_rows_of_group(0).then_inc(fb_types_done, 1)

                        def fb_window(w, first):
                            if layer == 2:
                                pe.wait_ge(fb_msgs, g + 1)
                            else:
                                pe.wait_ge(fb_gathered, g * (16 * C) + 16 * C * (layer * GROUPS + 1))
                            pe.wait_ge(fb_hot, g * WINDOWS + w + (layer * FB_ALL + 1))
                            if layer == 0:
                                window_count(0)
                            window_sum(layer, 0).then_inc(fb_summed, 1)
                        loop(pe, WINDOWS, fb_window)
                    loop(pe, GROUPS, fb_group)

                def node_products(h, left, weight, bias, bias_left):
                    for j in range(HALVES[h][1]):
                        at = slice(j * P, (j + 1) * P)
                        mm(post_ps[h][:, j, :], left[h][:, at], weight[:, :], True, False)
                        last = mm(post_ps[h][:, j, :], bias_left(h, at), rows_b[0:1, bias, :], False, True)
                    return last

                def post(i, first):
                    for h in range(2):
                        pe.wait_ge(mean_ready[h], i * 2 + (layer * 2 * STEPS + 2) if layer < 2
                                   else i + (4 * STEPS + 1))
                        if layer == 0 and not first:
                            pe.wait_ge(h_ready[h], i * 2 + (2 * STEPS - 1))
                        if layer > 0 and not first:
                            pe.wait_ge(post_read[h], i + (layer - 1) * STEPS)
                        weight, bias = ((w1, 0), (w2, 1), (wu, 3))[layer]
                        node_products(h, mean_T, weight, bias,
                                      (lambda h, at: has_in[h][0:1, at]) if layer < 2 else (lambda h, at: ones[0:1, :]))\
                            .then_inc(post_done[h], 1)
                loop(pe, STEPS, post, peel=True)

                if layer == 1:
                    def source_part(i, first):
                        for h, (_, n) in enumerate(HALVES):
                            pe.wait_ge(z_ready[h], i + 1)
                            if not first:
                                pe.wait_ge(tr_read[h], i)
                            for j in range(n):
                                last = nc.tensor.transpose(tr_ps[h][:, j * P:(j + 1) * P], hslot[h][:, j, :], ident[:, :])
                            last.then_inc(tr_done[h], 1)
                        for h in range(2):
                            pe.wait_ge(tr_read[h], i + 1)
                            if not first:
                                pe.wait_ge(h_ready[h], i * 2 + (4 * STEPS - 1))
                            node_products(h, mean_T, wm, 2, lambda h, at: ones[0:1, :]).then_inc(y_done[h], 1)
                    loop(pe, STEPS, source_part, peel=True)

        @block.vector
        def _(dve):
            steps = Steps(dve)
            V = nc.vector

            def chained(*instructions):
                for make in instructions:
                    steps.done(make())
                    steps.wait()

            def tile_stats(source, i, h):
                t0, n = HALVES[h]
                for j in range(n):
                    t = bass.ds(i * STEP + (t0 + j), 1)
                    last = V.bn_stats(stats[:, t, :], source[:, t, :])
                return last

            def mean_and_var():
                steps.wait()
                steps.done(V.tensor_tensor(mean[:, :], stats[:, :, 1], stats[:, :, 4], ALU.add))
                steps.done(V.tensor_tensor(std[:, :], stats[:, :, 1], stats[:, :, 4], ALU.subtract))
                steps.done(V.tensor_tensor(var[:, :], stats[:, :, 2], stats[:, :, 5], ALU.add))
                steps.wait()
                steps.done(V.tensor_single_scalar(mean[:, :], mean[:, :], 0.5, op=ALU.mult))
                steps.done(V.scalar_tensor_tensor(out=std[:, :], in0=std[:, :], scalar=0.25, in1=std[:, :],
                                                  op0=ALU.mult, op1=ALU.mult))
                steps.wait()
                V.scalar_tensor_tensor(out=var[:, :], in0=var[:, :], scalar=1.0 / F, in1=std[:, :],
                                       op0=ALU.mult, op1=ALU.add).then_inc(stats_ready, 1)

            def make_norm(k):
                dve.wait_ge(std_ready, k + 1)
                chained(lambda: V.reciprocal(rstd[k][:, :], std[:, :]))
                V.scalar_tensor_tensor(out=nmr[k][:, :], in0=mean[:, :], scalar=-1.0, in1=rstd[k][:, :],
                                       op0=ALU.mult, op1=ALU.mult).then_inc(norm_ready, 1)

            def later_parts(i, layer, value, before=lambda i: None):
                n = i + layer * STEPS
                for h in range(2):
                    dve.wait_ge(h_ready[h], i * 2 + (layer * 2 * STEPS + 2))
                    V.tensor_tensor(rslot[h], value[h], htab[:, tiles(i, h), part(0)], ALU.subtract).then_inc(rest_h[h], 1)
                for h in range(2):
                    dve.wait_ge(second_h[h], n + 1)
                    V.tensor_tensor(htab[:, tiles(i, h), part(2)], rslot[h], htab[:, tiles(i, h), part(1)], ALU.subtract)\
                        .then_inc(parts_ready[h], 1)
                    dve.wait_ge(parts_ready[h], n + 1)

            dve.wait_ge(edges_in, EDGE_LOADS)
            for s in range(2):
                V.tensor_copy(idx[s][:, :], src_all[:, (FIRST_GROUP + s) * C:(FIRST_GROUP + s + 1) * C])\
                    .then_inc(idx_ready[s], 1)
            per_group = lambda a: a[:, :].rearrange("p (g c) -> p g c", c=C)
            steps.done(V.tensor_tensor(per_group(rel), per_group(dst_all),
                                       base_all[:, :].unsqueeze(2).broadcast_to([P, GROUPS, C]), ALU.subtract))
            int_a, int_b = region_b[:, 0:BLOCK_COLS].bitcast(i32), region_b[:, BLOCK_COLS:2 * BLOCK_COLS].bitcast(i32)
            float_c = region_b[:, 2 * BLOCK_COLS:3 * BLOCK_COLS]
            types_i = far[:, 0:BLOCK_COLS].bitcast(i32)
            block_src, block_rel = src_all[:, 0:BLOCK_COLS], rel[:, 0:BLOCK_COLS]
            chained(lambda: V.tensor_single_scalar(first_tile[:, :], base_all[:, :], 7, op=ALU.arith_shift_right),
                    lambda: V.tensor_single_scalar(first_tile[:, :], first_tile[:, :], TILES - SPILL, op=ALU.min),
                    lambda: V.tensor_single_scalar(int_a, block_src, 7, op=ALU.arith_shift_right),
                    lambda: V.tensor_copy(tile_no[:, :], int_a),
                    lambda: V.tensor_single_scalar(int_a, block_src, P - 1, op=ALU.bitwise_and),
                    lambda: V.tensor_single_scalar(int_b, types_i, 7, op=ALU.logical_shift_left),
                    lambda: V.tensor_tensor(int_a, int_a, int_b, ALU.add),
                    lambda: V.tensor_copy(codes[:, 0, :], int_a),
                    lambda: V.tensor_single_scalar(float_c, block_rel, 0.0, op=ALU.is_ge),
                    lambda: V.scalar_tensor_tensor(out=float_c, in0=block_rel, scalar=float(WIN_B - 1), in1=float_c,
                                                   op0=ALU.is_le, op1=ALU.mult),
                    lambda: V.scalar_tensor_tensor(out=codes[:, 1, :], in0=block_rel, scalar=1.0, in1=float_c,
                                                   op0=ALU.add, op1=ALU.mult),
                    lambda: V.memset(scan_mask, 1.0),
                    lambda: V.memset(scan_mask[:, :, 0:1], 0.0))

            flat = lambda a: a.rearrange("p t c -> p (t c)")

            def sort_tiles(b, n):
                V.tensor_tensor(in_tile, tile_cols[:, :].unsqueeze(2).broadcast_to([P, T, BC]),
                                tile_no[:, bass.ds(b * BC, BC)].unsqueeze(1).broadcast_to([P, T, BC]), ALU.is_equal)\
                    .then_inc(in_tile_ready, 1)
                dve.wait_ge(in_tile_ready, n)
                steps.done(V.tensor_tensor_scan(flat(seen), flat(scan_mask), flat(in_tile), 0.0, ALU.mult, ALU.add))

            def sort_ranks(b, n):
                dve.wait_ge(before_done, n)
                steps.wait()
                chained(lambda: V.tensor_tensor(prod, seen, before_ps.unsqueeze(2).broadcast_to([P, T, BC]), ALU.add),
                        lambda: V.tensor_tensor(prod, prod, in_tile, ALU.mult),
                        lambda: V.tensor_reduce(out=rank1[:, bass.ds(b * BC, BC)], in_=prod.rearrange("p t c -> p c t"),
                                                axis=AX.X, op=ALU.add))

            def sort_codes(b, n):
                rank = rank1[:, bass.ds(b * BC, BC)]
                near, beyond, spill, slot = (sort_small[:, k, :] for k in range(4))
                two = lambda a: a.unsqueeze(1).broadcast_to([P, 2, BC])
                steps.done(V.tensor_single_scalar(near, rank, float(P), op=ALU.is_le))
                steps.done(V.tensor_single_scalar(beyond, rank, float(P), op=ALU.is_gt))
                steps.wait()
                steps.done(V.scalar_tensor_tensor(out=spill, in0=rank, scalar=float(2 * P), in1=beyond,
                                                  op0=ALU.is_le, op1=ALU.mult))
                steps.done(V.tensor_tensor(split_codes[0], codes[:, :, bass.ds(b * BC, BC)], two(near), ALU.mult))
                steps.wait()
                steps.done(V.tensor_tensor(split_codes[1], codes[:, :, bass.ds(b * BC, BC)], two(spill), ALU.mult))
                steps.done(V.scalar_tensor_tensor(out=slot, in0=spill, scalar=float(-P), in1=rank,
                                                  op0=ALU.mult, op1=ALU.add))
                steps.wait()
                own = dve.value_load(first_tile[0:1, bass.ds(b * GROUPS_STEP, 1)], min_val=0, max_val=TILES - SPILL)
                for k in range(2):
                    for at, m, code, tiles_of in ((k * BUCKETS, T, split_codes[0], in_tile),
                                                  (k * BUCKETS + T, SPILL, split_codes[1], in_tile[:, bass.ds(own, SPILL), :])):
                        V.tensor_tensor(coded[:, at:at + m, :], tiles_of,
                                        code[:, k, :].unsqueeze(1).broadcast_to([P, m, BC]), ALU.mult)
                V.tensor_tensor(slot_hot, columns1_h[:, :].unsqueeze(1).broadcast_to([P, BC, P]),
                                slot.unsqueeze(2).broadcast_to([P, BC, P]), ALU.is_equal).then_inc(coded_ready, 1)

            def sort_slots(b, n):
                dve.wait_ge(table_done, n)
                M = BUCKETS
                steps.done(V.tensor_copy(slot_dst[:, bass.ds(b * M, M)], table_ps[:, M:2 * M]))
                chained(lambda: V.tensor_copy(code_i[:, 0:M], table_ps[:, 0:M]),
                        lambda: V.tensor_single_scalar(code_i[:, M:2 * M], code_i[:, 0:M], P - 1, op=ALU.bitwise_and),
                        lambda: V.tensor_single_scalar(code_i[:, 2 * M:3 * M], code_i[:, 0:M], 7, op=ALU.arith_shift_right))
                V.tensor_copy(code_f, code_i[:, M:3 * M].rearrange("p (k t) -> p k t", k=2)).then_inc(code_f_ready, 1)

            def sort_turned(b, n, stored_before):
                dve.wait_ge(code_T_done, n)
                if stored_before is not None:
                    dve.wait_ge(code_T_stored, stored_before)
                V.tensor_copy(code_T, code_T_ps).then_inc(code_T_ready, 1)
            SORT_STEPS = 1 + 3 + 6 + 4

            dve.wait_ge(consts, CONSTS)
            sort_tiles(0, 1)

            dve.wait_ge(x_in, 16)

            def x_stats(i, first):
                for h in range(2):
                    steps.done(tile_stats(xres, i, h))
            steps.loop(STEPS, 2, x_stats)
            mean_and_var()
            sort_ranks(0, 1)
            sort_codes(0, 1)
            make_norm(0)
            sort_slots(0, 1)

            chained(lambda: V.tensor_single_scalar(part_i[:, 1:2], part_i[:, 0:1], 4, op=ALU.arith_shift_right),
                    lambda: V.tensor_copy(third[:, :], part_i[:, 1:2]),
                    lambda: V.tensor_single_scalar(part_i[:, 1:2], part_i[:, 0:1], TYPES - 1, op=ALU.bitwise_and),
                    lambda: V.tensor_copy(type_no[:, :], part_i[:, 1:2]))
            for k in range(K3):
                steps.done(V.tensor_single_scalar(masks[:, k:k + 1], third[:, :], float(k), op=ALU.is_equal))
            sort_turned(0, 1, None)
            dve.wait_ge(setup_done, 1)
            product = setup_ps[0:K3 * TYPES, 0:F]
            chained(lambda: V.tensor_copy(type_p[:, 0, :], product),
                    lambda: V.tensor_tensor(type_f[:, 0, :], product, type_p[:, 0, :], ALU.subtract),
                    lambda: V.tensor_copy(type_p[:, 1, :], type_f[:, 0, :]),
                    lambda: V.tensor_tensor(type_p[:, 2, :], type_f[:, 0, :], type_p[:, 1, :], ALU.subtract),
                    lambda: V.tensor_scalar(type_f[:, 0, :], type_p[:, 0, :], masks[:, 0:1], None, ALU.mult),
                    lambda: V.scalar_tensor_tensor(out=type_f[:, 1, :], in0=type_p[:, 1, :], scalar=masks[:, 1:2],
                                                   in1=type_f[:, 0, :], op0=ALU.mult, op1=ALU.add))
            V.scalar_tensor_tensor(out=type_rows[:, :], in0=type_p[:, 2, :], scalar=masks[:, 2:3], in1=type_f[:, 1, :],
                                   op0=ALU.mult, op1=ALU.add).then_inc(type_rows_ready, 1)
            loop(dve, STEPS, lambda i, first: later_parts(i, 0, hslot))
            for h in range(2):
                dve.wait_ge(h_ready[h], 2 * STEPS)
            steps.done(V.memset(cnt, 0.0))

            def make_hot(layer, s, cols):
                to = hot[s][:, :, :] if layer == 2 else hot_b[s]
                return V.tensor_tensor(to, (columns if layer == 2 else columns_b)[:, :].unsqueeze(1).broadcast_to([P, C, P]),
                                       cols.unsqueeze(2).broadcast_to([P, C, P]), ALU.is_equal)

            def make_types_hot(s):
                return V.tensor_scalar(types_hot[s], types_in[s], type_no[:, 0:1], None, ALU.is_equal)

            far_n = None
            for layer in range(LAYERS):
                for h in range(2):
                    if layer > 0:
                        dve.wait_ge(mean_ready[h], layer * 2 * STEPS)
                chained(lambda: V.memset(agg[:, :], 0.0))

                def main(b, first):
                    c = Count(dve, layer, b, first, [(16, 16), (16 * C, 16 * C)] + [
                        [(1, 2), (32, 32)] + [(BUCKETS // R, k) for k in range(BUCKETS // R + 1)],
                        [(BUCKETS // R, k) for k in range(BUCKETS // R + 1)],
                        [(32, 32 - 2 * B * 16)] + [(U, k - 2 * B * U) for k in range(-1, U + 1)]][layer])

                    def source_hot(u):
                        dve.wait_ge(src_loaded[u], c.here(16) if layer < 2 else c(32, 32 - 2 * B * 16))
                        s, m = u % 2, len(UNITS[u])
                        if layer == 2 and not (first and u < 2):
                            dve.wait_ge(unit_picked, c.unit(u - 2, since=2))
                        elif layer < 2 and not (c.none and u < 2):
                            t = UNITS[u - 2][-1] - (0 if u >= 2 else BUCKETS)
                            dve.wait_ge(pick_done[t % R], c.bucket(t))
                        if layer == 2:
                            V.tensor_scalar(btypes_hot[s][:, 0:m * P], btypes_in[s][:, 0:m * P], type_no[:, 0:1], None,
                                            ALU.is_equal)
                        V.tensor_scalar(src_hot[s][:, 0:m * P], src_in[s][:, 0:m * P], part_no[:, 0:1], None, ALU.is_equal)\
                            .then_inc(src_hot_ready, 1)

                    def destination_hot(u):
                        if not (c.none and u < 2):
                            dve.wait_ge(unit_summed, c.unit(u - 2))
                        to, numbers = (dst_hot_f, columns1) if layer == 2 else (dst_hot, columns1_b)
                        for j, t in enumerate(UNITS[u]):
                            last = V.tensor_scalar(to[u % 2][:, j, :], numbers[:, :],
                                                   slot_dst[:, bass.ds(b * BUCKETS + t, 1)], None, ALU.is_equal)
                        last.then_inc(dst_hot_ready, 1)

                    def window_add(n, at, size, ps, cps):
                        base = dve.value_load(base_all[0:1, bass.ds(at, 1)], min_val=0, max_val=N)
                        before = c.before() if n == 0 else c.here()
                        window = bass.ds(base, size)
                        if not (c.none and n == 0):
                            dve.wait_ge(added[n - 1], before)
                        V.tensor_tensor(agg[:, window], agg[:, window], ps, ALU.add).then_inc(added[n], 1)
                        if layer == 0:
                            if not (c.none and n == 0):
                                dve.wait_ge(counted[n - 1], before)
                            V.tensor_tensor(cnt[:, window], cnt[:, window], cps, ALU.add).then_inc(counted[n], 1)

                    def group_hot(gi):
                        g = b * GROUPS_STEP + (FIRST_GROUP + gi)
                        if not (c.none and gi < 2):
                            dve.wait_ge(summed[(gi + 2) % 4], c.before() if gi < 2 else c.here())
                        make_hot(layer, gi % 2, rel[:, bass.ds(g * C, C)]).then_inc(hot_ready[gi], 1)
                        if layer == 2:
                            dve.wait_ge(types_loaded[gi], b * 16 + 16)
                            if gi > 1 or not first:
                                dve.wait_ge(types_done[(gi + 2) % 4], b if gi < 2 else b + 1)
                            make_types_hot(gi % 2).then_inc(types_hot_ready[gi], 1)

                    def group_rows(gi):
                        g = b * GROUPS_STEP + (FIRST_GROUP + gi)
                        dve.wait_ge(gathered[gi], c.here(16 * C))
                        V.tensor_copy(idx[gi % 2][:, :], src_all[:, bass.ds((g + 2) * C, C)])\
                            .then_inc(idx_ready[(gi + 2) % 4], 1)
                        if layer == 2:
                            dve.wait_ge(types_done[gi], b + 1)
                            V.tensor_tensor(rows_f[gi % 2], type_ps, rows_f[gi % 2], ALU.add).then_inc(pre_ready[gi], 1)

                    def group_add(gi):
                        dve.wait_ge(summed[gi], c.here())
                        window_add(gi, b * GROUPS_STEP + (FIRST_GROUP + gi), WIN_G, sum_ps[gi % 2], cnt_ps[gi % 2])

                    hot_at, add_at = (GROUP_TYPES, GROUP_AFTER) if layer == 2 else (GROUP_AFTER, GROUP_AFTER)
                    source_hot(0)
                    for u in range(U):
                        if u + 1 < U:
                            source_hot(u + 1)
                        if u in hot_at:
                            group_hot(hot_at.index(u))
                        destination_hot(u)
                        if layer == 0:
                            n = SORT_N(c)
                            if u == 0:
                                sort_tiles(b + 1, n)
                            elif u == 1:
                                sort_ranks(b + 1, n)
                            elif u == 2:
                                sort_codes(b + 1, n)
                            elif u == 3:
                                sort_slots(b + 1, n)
                            elif u == 4:
                                sort_turned(b + 1, n, c(32, 32))
                        if u in hot_at:
                            group_rows(hot_at.index(u))
                        if u - 1 in add_at:
                            group_add(add_at.index(u - 1))
                    group_add(3)
                    dve.wait_ge(unit_summed, c.unit(U - 1))
                    window_add(4, b * GROUPS_STEP, WIN_B, bsum_ps, bcnt_ps)
                if layer == 0:
                    steps.loop(B, SORT_STEPS, main, peel=True)
                else:
                    loop(dve, B, main, peel=layer != 1)
                dve.wait_ge(added[4], (layer + 1) * B)
                dve.wait_ge(counted[4], B)

                if layer == 0:
                    mask = region_b[:, 0:GROUPS * C]
                    spare = region_b[:, GROUPS * C:GROUPS * C + B * BC]
                    halves = ((slice(0, B * BC), WIN_B), (slice(B * BC, GROUPS * C), WIN_G))
                    steps.wait()
                    chained(lambda: V.tensor_single_scalar(mask, rel[:, :], 0.0, op=ALU.is_lt))
                    for at, size in halves:
                        steps.done(V.scalar_tensor_tensor(out=far[:, at], in0=rel[:, at], scalar=float(size - 1),
                                                          in1=mask[:, at], op0=ALU.is_gt, op1=ALU.max))
                    steps.wait()
                    at = halves[0][0]
                    own = mask[:, at].rearrange("p (g c) -> p g c", c=C)
                    in_block = lambda a: a[:, at]
                    chained(lambda: V.scalar_tensor_tensor(out=far[:, at], in0=rank1[:, at], scalar=float(2 * P),
                                                           in1=far[:, at], op0=ALU.is_gt, op1=ALU.max),
                            lambda: V.tensor_tensor(own, in_block(tile_no).rearrange("p (g c) -> p g c", c=C),
                                                    first_tile[:, 0:B * GROUPS_STEP].unsqueeze(2)
                                                    .broadcast_to([P, B * GROUPS_STEP, C]), ALU.subtract),
                            lambda: V.tensor_single_scalar(spare, mask[:, at], 0.0, op=ALU.is_lt),
                            lambda: V.scalar_tensor_tensor(out=spare, in0=mask[:, at], scalar=float(SPILL - 1), in1=spare,
                                                           op0=ALU.is_gt, op1=ALU.max),
                            lambda: V.scalar_tensor_tensor(out=spare, in0=rank1[:, at], scalar=float(P), in1=spare,
                                                           op0=ALU.is_gt, op1=ALU.mult),
                            lambda: V.tensor_tensor(far[:, at], far[:, at], spare, ALU.max),
                            lambda: V.scalar_tensor_tensor(out=mask, in0=dst_all[:, :], scalar=1.0, in1=far[:, :],
                                                           op0=ALU.add, op1=ALU.mult),
                            lambda: V.tensor_single_scalar(far[:, :], mask, -1.0, op=ALU.add),
                            lambda: V.reduce_max(far_max[:, :], far[:, :], axis=AX.X))
                    V.tensor_single_scalar(far_one[:, :], far_max[:, :], 0.0, op=ALU.is_ge).then_inc(far_ready, 1)
                    dve.wait_ge(setup_done, 2)
                    V.tensor_copy(flag[0:1, 0:1], setup_ps[0:1, F:F + 1]).then_inc(far_known, 1)
                    dve.wait_ge(far_known, 1)
                    far_n = dve.value_load(flag[0:1, 0:1], min_val=0, max_val=P)

                with dve.If(far_n > 0):
                    ADDS = 3 * WINDOWS + 1

                    def fb_group(g, first):
                        V.tensor_copy(fb_idx_cols[:, :], src_all[:, bass.ds(g * C, C)]).then_inc(fb_idx, 1)
                        if layer == 2:
                            dve.wait_ge(fb_types_in, g * 16 + 16)
                            make_types_hot(0).then_inc(fb_types_hot, 1)
                        dve.wait_ge(fb_gathered, g * (16 * C) + 16 * C * (layer * GROUPS + 1))
                        if layer == 2:
                            dve.wait_ge(fb_types_done, g + 1)
                            V.tensor_tensor(rows_f[0], type_ps, rows_f[0], ALU.add).then_inc(fb_pre, 1)
                        V.tensor_copy(far_w[:, :], far[:, bass.ds(g * C, C)]).then_inc(fb_added, 1)

                        def fb_window(w, first):
                            at = g * WINDOWS + w + (layer * FB_ALL + 1)
                            dve.wait_ge(fb_added, g * ADDS + w * 3 + (layer * ADDS * GROUPS + 1))
                            make_hot(layer, 0, far_w[:, :]).then_inc(fb_hot, 1)
                            dve.wait_ge(fb_hot, at)
                            V.tensor_single_scalar(far_w[:, :], far_w[:, :], float(-P), op=ALU.add).then_inc(fb_added, 1)
                            dve.wait_ge(fb_summed, at)
                            window = bass.ds(w * P, P)
                            V.tensor_tensor(agg[:, window], agg[:, window], sum_ps[0], ALU.add).then_inc(fb_added, 1)
                            if layer == 0:
                                V.tensor_tensor(cnt[:, window], cnt[:, window], cnt_ps[0], ALU.add).then_inc(fb_added, 1)
                            else:
                                dve.engine_nop().then_inc(fb_added, 1)
                        loop(dve, WINDOWS, fb_window)
                    loop(dve, GROUPS, fb_group)
                    dve.wait_ge(fb_added, (layer + 1) * ADDS * GROUPS)

                def post(i, first):
                    for h, (_, n) in enumerate(HALVES):
                        at = nodes(i, h)
                        if layer == 2 and first:
                            dve.wait_ge(y_done[h], STEPS)
                        elif layer > 0 or not first:
                            dve.wait_ge(post_done[h], i + layer * STEPS)
                        if layer == 0:
                            chained(lambda: V.tensor_single_scalar(mean_T[h], cnt[:, at], 1.0, op=ALU.max),
                                    lambda: V.reciprocal(mean_T[h], mean_T[h]))
                            if not first:
                                dve.wait_ge(rinv_stored[h], i * 16)
                            V.scalar_tensor_tensor(out=rinv[h], in0=cnt[:, at], scalar=1.0, in1=mean_T[h],
                                                   op0=ALU.min, op1=ALU.mult).then_inc(rinv_ready[h], 1)
                            dve.wait_ge(rinv_ready[h], i + 1)
                        else:
                            dve.wait_ge(rinv_loaded[h], i * 16 + 16 * ((layer - 1) * STEPS + 1))
                        V.tensor_tensor(mean_T[h], agg[:, at], rinv[h], ALU.mult).then_inc(mean_ready[h], 1)
                        if layer < 2:
                            V.tensor_single_scalar(has_in[h], rinv[h][0:1, :], 0.0, op=ALU.is_gt).then_inc(mean_ready[h], 1)
                    if layer == 0:
                        later_parts(i, 1, hslot)
                        return
                    to = xres if layer == 1 else hres
                    dve.wait_ge(x_in, 32)
                    for h, (_, n) in enumerate(HALVES):
                        dve.wait_ge(post_done[h], i + (layer * STEPS + 1))
                        if layer == 2:
                            dve.wait_ge(h_ready[h], i + (6 * STEPS + 1))
                        V.tensor_tensor(to[:, tiles(i, h), :], post_ps[h][:, 0:n, :],
                                        xres[:, tiles(i, h), :] if layer == 1 else hslot[h], ALU.add).then_inc(post_read[h], 1)
                        dve.wait_ge(post_read[h], i + ((layer - 1) * STEPS + 1))
                        steps.done(tile_stats(to, i, h))
                if layer == 0:
                    steps.loop(STEPS, 4, post, peel=True)
                    continue
                steps.loop(STEPS, 2, post, peel=True)
                mean_and_var()
                make_norm(layer)

                if layer == 1:
                    def transposed(i, first):
                        for h, (_, n) in enumerate(HALVES):
                            dve.wait_ge(tr_done[h], i + 1)
                            if not first:
                                dve.wait_ge(y_done[h], i)
                            V.tensor_copy(mean_T[h], tr_ps[h][:, 0:n * P]).then_inc(tr_read[h], 1)
                        later_parts(i, 2, oslot)
                    loop(dve, STEPS, transposed, peel=True)
                else:
                    def scale(i, first):
                        for h, (_, n) in enumerate(HALVES):
                            V.tensor_tensor(xres[:, tiles(i, h), :], xres[:, tiles(i, h), :],
                                            b_all[:, :].unsqueeze(1).broadcast_to([P, n, F]), ALU.add)
                            dve.wait_ge(z_ready[h], i + (STEPS + 1))
                            if not first:
                                dve.wait_ge(out_stored[h], i * 16)
                            V.tensor_tensor(oslot[h], rslot[h], g_all[:, :].unsqueeze(1).broadcast_to([P, n, F]), ALU.mult)\
                                .then_inc(scaled[h], 1)
                    loop(dve, STEPS, scale, peel=True)


def kernel(**inputs):
    import numpy as np
    import concourse.bacc as bacc
    from concourse import mybir
    from concourse.bass_utils import run_bass_kernel_spmd

    a = {k: np.ascontiguousarray(v) for k, v in inputs.items()}
    N, F = a["x"].shape
    E = a["src"].shape[0]
    assert (GROUPS - 1) * GE < E <= GROUPS * GE
    rows = -(-N // P) * P
    types = a["L1_gnn_edge_emb_W"].shape[0]

    def padded(e, fill):
        return np.concatenate([e.astype(np.int32), np.full(GROUPS * GE - E, fill, np.int32)])

    def by_partition(e):
        return np.ascontiguousarray(e.reshape(GROUPS * C, P).T)

    dst = padded(a["dst"], N)
    etype = padded(a["edge_type_16"], 0)
    blocks = GROUPS // 2
    firsts = np.arange(GROUPS)
    firsts = np.where(firsts < blocks, firsts // GROUPS_STEP * GROUPS_STEP, firsts) * GE
    arrays = {
        "x": np.concatenate([a["x"], np.zeros((rows - N, F), a["x"].dtype)]),
        "src": by_partition(padded(a["src"], 0)),
        "dst": by_partition(dst),
        "first_dst": dst[firsts],
        "etype_cols": by_partition(etype),
        "etype": np.broadcast_to(etype.reshape(GROUPS, 1, GE), (GROUPS, 3 * types, GE)),
        "W1T": a["L0_gnn_W1"].T, "b1": a["L0_gnn_b1"], "W2T": a["L0_gnn_W2"].T, "b2": a["L0_gnn_b2"],
        "embT": a["L1_gnn_edge_emb_W"].T, "msgWT": a["L1_gnn_msg_W"].T, "msg_b": a["L1_gnn_msg_b"],
        "updWT": a["L1_gnn_upd_W"].T, "upd_b": a["L1_gnn_upd_b"], "ln_g": a["L1_gnn_ln_g"], "ln_b": a["L1_gnn_ln_b"],
    }
    arrays = {k: np.ascontiguousarray(v) for k, v in arrays.items()}
    nc = bacc.Bacc("TRN2", target_bir_lowering=False, num_devices=1)
    args = {k: nc.dram_tensor(f"in_{k}", v.shape, mybir.dt.from_np(v.dtype), kind="ExternalInput").ap()
            for k, v in arrays.items()}
    out = nc.dram_tensor("out_dram", (rows, F), mybir.dt.float32, kind="ExternalOutput").ap()
    gnn_program(nc, N, **args, out=out)
    r = run_bass_kernel_spmd(nc, [{f"in_{k}": v for k, v in arrays.items()}], core_ids=[0])
    return r.results[0]["out_dram"][:N]
```

```python
import concourse.bass as bass
from concourse import mybir
from contextlib import ExitStack

P = 128
C = 8
GE = C * P
GROUPS_STEP = 4
STEPS_MAIN = 13
BLOCK_C = GROUPS_STEP * C
GROUPS = 2 * STEPS_MAIN * GROUPS_STEP


def gnn_program(nc, N, x, src, dst, first_dst, etype_cols, etype, W1T, b1, W2T, b2, embT, msgWT, msg_b,
                updWT, upd_b, ln_g, ln_b, out):
    fp32 = mybir.dt.float32
    fp16 = mybir.dt.float16
    bf16 = mybir.dt.bfloat16
    i32 = mybir.dt.int32
    ALU = mybir.AluOpType
    ACT = mybir.ActivationFunctionType
    AX = mybir.AxisListType

    F = x.shape[1]
    TILES = x.shape[0] // P
    SPILL = 3
    BUCKETS = TILES + SPILL
    ETD, TYPES = embT.shape
    LAYERS = 3
    B = STEPS_MAIN
    FIRST_GROUP = B * GROUPS_STEP
    BLOCK_COLS = (B + 1) * BLOCK_C
    WIN_G, WIN_B = P, 2 * P
    WINDOWS = TILES + 1
    COLS = WINDOWS * P + P
    UNITS = []
    while sum(map(len, UNITS)) < BUCKETS:
        at = sum(map(len, UNITS))
        UNITS.append(range(at, at + (7 if len(UNITS) < 4 else 6)))
    U, J = len(UNITS), 7
    R = 13
    assert sum(map(len, UNITS)) == BUCKETS == 4 * R and U % 2 == 0
    assert N + WIN_G <= COLS and N - 1 + WIN_B <= COLS
    HALVES = ((0, 4), (4, 3))
    STEP = 7
    STEPS = TILES // STEP
    EPS = 1e-5
    K3 = 3

    ctx = ExitStack()
    with ctx:
        def sb(name, shape, dt=fp32):
            return ctx.enter_context(nc.sbuf_tensor(name, shape, dt))

        def sem(name):
            return ctx.enter_context(nc.semaphore(name))

        def sems(name, n):
            return [sem(f"{name}{k}") for k in range(n)]

        tab = [nc.dram_tensor(f"table{k}", (TILES * P, F if k == 2 else K3 * F), fp32 if k == 2 else bf16,
                              kind="Internal").ap() for k in range(LAYERS)]
        tab_v = [t.rearrange("(t p) f -> p t f", p=P) for t in tab]
        src_tab = nc.dram_tensor("src_tab", (B + 1, BUCKETS, P), bf16, kind="Internal").ap()
        type_tab = nc.dram_tensor("type_tab", (B + 1, BUCKETS, P), bf16, kind="Internal").ap()
        degree_tab = nc.dram_tensor("degree_tab", (P, TILES), fp32, kind="Internal").ap()
        rinv_tab = nc.dram_tensor("rinv_tab", (P, TILES), fp32, kind="Internal").ap()
        one_row = lambda t: t.rearrange("p t -> (p t)").rearrange("(a n) -> a n", a=1)
        x_v = x.rearrange("(t p) f -> p t f", p=P)
        out_v = out.rearrange("(t p) f -> p t f", p=P)

        src_all = sb("src_all", [P, (GROUPS + 2) * C], i32)
        dst_all = sb("dst_all", [P, GROUPS * C], i32)
        base_all = sb("base_all", [P, GROUPS], i32)
        rel = sb("rel", [P, GROUPS * C])
        far = sb("far", [P, GROUPS * C])
        tile_no = sb("tile_no", [P, BLOCK_COLS], fp16)
        codes = sb("codes", [P, 2, BLOCK_COLS], fp16)
        first_tile = sb("first_tile", [P, GROUPS], i32)
        rank1 = sb("rank1", [P, BLOCK_COLS])
        slot_dst = sb("slot_dst", [P, (B + 1) * BUCKETS])
        far_max = sb("far_max", [P, 1])
        far_one = sb("far_one", [P, 1])
        flag = sb("flag", [1, 1], i32)
        far_w = sb("far_w", [P, C])
        fb_idx_cols = sb("fb_idx_cols", [P, C], i32)
        columns = sb("columns", [P, P])
        columns_b = sb("columns_b", [P, P], bf16)
        columns1_b = sb("columns1_b", [P, WIN_B], bf16)
        columns1 = sb("columns1", [P, WIN_B])
        columns1_h = sb("columns1_h", [P, P], fp16)
        part_no = sb("part_no", [P, 1])
        part_i = sb("part_i", [K3 * TYPES, 2], i32)
        type_no = sb("type_no", [K3 * TYPES, 1])
        third = sb("third", [K3 * TYPES, 1])
        masks = sb("masks", [K3 * TYPES, K3])
        ones = sb("ones", [P, P])
        ones_b = sb("ones_b", [P, P], bf16)
        ident = sb("ident", [P, P])
        below = sb("below", [P, P], fp16)
        eps = sb("eps", [P, 1])
        w1 = sb("w1", [P, F])
        w2 = sb("w2", [P, F])
        wm = sb("wm", [P, F])
        wt = sb("wt", [ETD, F])
        wu = sb("wu", [P, F])
        emb = sb("emb", [ETD, K3, TYPES])
        bias_in = sb("bias_in", [K3, 4, F])
        bias_parts = sb("bias_parts", [K3, 4, F], bf16)
        bias_masks = sb("bias_masks", [K3, K3])
        g_all = sb("g_all", [P, F])
        b_all = sb("b_all", [P, F])
        type_f = sb("type_f", [K3 * TYPES, 2, F])
        type_p = sb("type_p", [K3 * TYPES, K3, F], bf16)
        type_rows = sb("type_rows", [K3 * TYPES, F], bf16)
        idx = [sb(f"idx{s}", [P, C], i32) for s in range(2)]
        rows = [sb(f"rows{s}", [P, C, K3 * F], bf16) for s in range(2)]
        rows_f = [r[:, :, :].rearrange("p c f -> p (c f)")[:, 0:2 * GE].bitcast(fp32).rearrange("p (c f) -> p c f", f=F)
                  for r in rows]
        hot = [sb(f"hot{s}", [P, C, P]) for s in range(2)]
        hot_b = [h[:, :, :].rearrange("p c f -> p (c f)").bitcast(bf16)[:, 0:GE].rearrange("p (c f) -> p c f", f=P)
                 for h in hot]
        src_in = [sb(f"src_in{s}", [P, J * P], bf16) for s in range(2)]
        src_hot = [sb(f"src_hot{s}", [P, J * P], bf16) for s in range(2)]
        agg = sb("agg", [P, COLS])
        x_or_cnt = sb("x_or_cnt", [P, COLS])
        cnt = x_or_cnt[:, :]
        xres = x_or_cnt[:, 0:TILES * F].rearrange("p (t f) -> p t f", f=F)
        htab = sb("htab", [P, TILES, K3 * F], bf16)
        stats = sb("stats", [P, TILES, 6])
        mean = sb("mean", [P, TILES])
        var = sb("var", [P, TILES])
        std = sb("std", [P, TILES])
        degree = sb("degree", [P, TILES])
        at_least_1 = sb("at_least_1", [P, TILES])
        rstd = [sb(f"rstd{k}", [P, TILES]) for k in range(3)]
        nmr = [sb(f"nmr{k}", [P, TILES]) for k in range(3)]

        def carve(region, at, shape, dt, size):
            n = 1
            for d in shape[1:]:
                n *= d
            a = region[0:shape[0], at // 4:(at + n * size + 3) // 4]
            a = a if dt == fp32 else a.bitcast(dt)[:, 0:n]
            if len(shape) == 3:
                a = a.rearrange("p (a b) -> p a b", b=shape[2])
            return a, at + (n * size + 3) // 4 * 4

        def carver(region):
            at = [0]

            def take(shape, dt=fp32, size=4):
                a, at[0] = carve(region, at[0], shape, dt, size)
                return a
            return take

        region_a = sb("region_a", [P, 6300])
        take = carver(region_a)
        dst_hot = [take([P, J, WIN_B], bf16, 2) for _ in range(2)]
        picked = [take([P, J, K3 * F], bf16, 2) for _ in range(2)]
        take = carver(region_a)
        dst_hot_f = [take([P, J, WIN_B]) for _ in range(2)]
        messages = [take([P, J, F]) for _ in range(2)]
        take = carver(region_a)
        mean_T = [take([P, n * P]) for _, n in HALVES]
        hslot = [take([P, n, F]) for _, n in HALVES]
        rslot = [take([P, n, F]) for _, n in HALVES]
        oslot = [take([P, n, F]) for _, n in HALVES]
        has_in = [take([K3, n * P], bf16, 2) for _, n in HALVES]
        rinv = [take([P, n * P]) for _, n in HALVES]
        region_b = sb("region_b", [P, 7500])
        take = carver(region_b)
        BC, T = BLOCK_C, TILES
        in_tile = take([P, T, BC], fp16, 2)
        seen = take([P, T, BC], fp16, 2)
        prod = take([P, T, BC], fp16, 2)
        scan_mask = take([P, T, BC], fp16, 2)
        coded = take([P, 2 * BUCKETS, BC], fp16, 2)
        slot_hot = take([P, BC, P], fp16, 2)
        code_i = take([P, 3 * BUCKETS], i32)
        code_f = take([P, 2, BUCKETS])
        code_T = take([BUCKETS, 2 * P], bf16, 2)
        sort_small = take([P, 4, BC])
        split_codes = [take([P, 2, BC], fp16, 2) for _ in range(2)]
        take = carver(region_b)
        take([P, 4000])
        bias_f = [take([K3, 4, F]) for _ in range(2)]
        bias_p = [take([K3, 4, F], bf16, 2) for _ in range(K3)]
        take = carver(region_b)
        types_in = [take([K3 * TYPES, GE], i32) for _ in range(2)]
        types_hot = [take([K3 * TYPES, GE], bf16, 2) for _ in range(2)]
        btypes_in = [take([K3 * TYPES, J * P], bf16, 2) for _ in range(2)]
        btypes_hot = [take([K3 * TYPES, J * P], bf16, 2) for _ in range(2)]
        tile_cols = sb("tile_cols", [P, T], fp16)

        banks = ctx.enter_context(nc.psum_tensor("banks", [P, 8, 512], fp32))
        sum_ps = [banks[:, 0, 2 * s * P:(2 * s + 1) * P] for s in range(2)]
        cnt_ps = [banks[:, 0, (2 * s + 1) * P:(2 * s + 2) * P] for s in range(2)]
        bsum_ps = banks[:, 1, 0:WIN_B]
        bcnt_ps = banks[:, 2, 0:WIN_B]
        before_ps = banks[:, 3, 0:T]
        table_ps = banks[:, 3, 64:64 + 2 * BUCKETS]
        code_T_ps = banks[0:BUCKETS, 3, 256:512]
        pick_ps = [banks[:, 4 + k, 0:K3 * F] for k in range(4)]
        type_ps = banks[:, 2:4, :].rearrange("p b (c f) -> p (b c) f", f=F)
        message_ps = [banks[:, 4 + 2 * s:6 + 2 * s, :].rearrange("p b (t f) -> p (b t) f", f=F) for s in range(2)]
        post_ps = [banks[:, 4 + h, :].rearrange("p (t f) -> p t f", f=F) for h in range(2)]
        tr_ps = [banks[:, 6 + h, :] for h in range(2)]
        setup_ps = banks[:, 7, :]

        edges_in = sem("edges_in")
        x_in = sem("x_in")
        weights_in = sem("weights_in")
        consts = sem("consts")
        cleared = sem("cleared")
        dve_step = sem("dve_step")
        far_ready = sem("far_ready")
        far_known = sem("far_known")
        setup_done = sem("setup_done")
        type_rows_ready = sem("type_rows_ready")
        idx_ready = sems("idx_ready", 4)
        gathered = sems("gathered", 4)
        hot_ready = sems("hot_ready", 4)
        summed = sems("summed", 4)
        types_loaded = sems("types_loaded", 4)
        types_hot_ready = sems("types_hot_ready", 4)
        types_done = sems("types_done", 4)
        pre_ready = sems("pre_ready", 4)
        msgs_ready = sems("msgs_ready", 4)
        added = sems("added", 5)
        counted = sems("counted", 5)
        src_loaded = sems("src_loaded", U)
        src_hot_ready = sem("src_hot_ready")
        dst_hot_ready = sem("dst_hot_ready")
        unit_picked = sem("unit_picked")
        unit_summed = sem("unit_summed")
        pick_done = sems("pick_done", R)
        pick_read = sems("pick_read", R)
        messages_ready = sem("messages_ready")
        in_tile_ready = sem("in_tile_ready")
        before_done = sem("before_done")
        coded_ready = sem("coded_ready")
        table_done = sem("table_done")
        code_f_ready = sem("code_f_ready")
        code_T_done = sem("code_T_done")
        code_T_ready = sem("code_T_ready")
        code_T_stored = sem("code_T_stored")
        fb_idx = sem("fb_idx")
        fb_gathered = sem("fb_gathered")
        fb_types_in = sem("fb_types_in")
        fb_types_hot = sem("fb_types_hot")
        fb_types_done = sem("fb_types_done")
        fb_pre = sem("fb_pre")
        fb_msgs = sem("fb_msgs")
        fb_hot = sem("fb_hot")
        fb_summed = sem("fb_summed")
        fb_added = sem("fb_added")
        sums_cleared = sem("sums_cleared")
        degree_ready = sem("degree_ready")
        degree_moved = sem("degree_moved")
        rinv_loaded = sems("rinv_loaded", 2)
        mean_ready = sems("mean_ready", 2)
        post_done = sems("post_done", 2)
        post_read = sems("post_read", 2)
        stats_ready = sem("stats_ready")
        std_ready = sem("std_ready")
        norm_ready = sem("norm_ready")
        h_ready = sems("h_ready", 2)
        rest_h = sems("rest_h", 2)
        second_h = sems("second_h", 2)
        parts_ready = sems("parts_ready", 2)
        tr_done = sems("tr_done", 2)
        tr_read = sems("tr_read", 2)
        y_done = sems("y_done", 2)
        z_ready = sems("z_ready", 2)
        scaled = sems("scaled", 2)
        out_ready = sems("out_ready", 2)
        stored = sems("stored", 2)
        out_stored = sems("out_stored", 2)

        EDGE_LOADS = 5 * 16
        WEIGHT_LOADS = 14 * 16
        CONSTS = 13
        FB_ALL = GROUPS * WINDOWS

        block = ctx.enter_context(nc.Block())

        def loop(eng, n, step, peel=False):
            if peel:
                step(0, True)
            with eng.Fori(1 if peel else 0, n) as i:
                step(i, False)

        class Steps:

            def __init__(self, eng):
                self.eng, self.base, self.n = eng, 0, 0

            def done(self, ins):
                ins.then_inc(dve_step, 1)
                self.n += 1

            def wait(self):
                self.eng.wait_ge(dve_step, self.base + self.n)

            def loop(self, n, per, step, peel=False):
                start = self.base + self.n

                def one(i, first):
                    self.base, self.n = i * per + start, 0
                    step(i, first)
                    assert self.n == per, self.n
                loop(self.eng, n, one, peel)
                self.base, self.n = start + n * per, 0

        class Count:

            def __init__(self, eng, layer, b, first, own=()):
                self.eng, self.layer, self.b, self.first = eng, layer, b, first
                self.K = b + layer * B
                self.have = {}
                self.none = first and layer == 0
                if not first:
                    for times, plus in [(1, 0), (1, 1)] + [(U, k) for k in range(-1, U + 1)] + list(own):
                        self(times, plus)

            def __call__(self, times, plus):
                if self.first:
                    return times * self.K + plus
                if (times, plus) not in self.have:
                    self.have[times, plus] = self.eng.snap(self.eng.to_reg(self.K * times + plus))
                return self.have[times, plus]

            def unit(self, u, last_step=False, since=0):
                return self(U, u + 1 - (U if last_step else 0) - since * B * U)

            def bucket(self, t):
                return self(BUCKETS // R, t // R + 1)

            def here(self, times=1):
                return self(times, times)

            def before(self, times=1):
                return self(times, 0)

        def tiles(i, h):
            t0, n = HALVES[h]
            return bass.ds(i * STEP + t0, n)

        def nodes(i, h):
            t0, n = HALVES[h]
            return bass.ds(i * (STEP * P) + t0 * P, n * P)

        part = lambda k: slice(k * F, (k + 1) * F)
        GROUP_AFTER = (1, 3, 5, 7)
        GROUP_HOT = (0, 2, 4, 6)
        SORT_N = lambda c: c(1, 2)
        hres = htab[:, :, 0:2 * F].bitcast(fp32)


        @block.sync
        def _(sp):
            sp.dma_start(src_all[:, 0:GROUPS * C], src).then_inc(edges_in, 16)
            sp.dma_start(src_all[:, GROUPS * C:], src[:, FIRST_GROUP * C:(FIRST_GROUP + 2) * C]).then_inc(edges_in, 16)
            sp.dma_start(dst_all[:, :], dst).then_inc(edges_in, 16)
            sp.dma_start(base_all[:, :], first_dst.partition_broadcast(P)).then_inc(edges_in, 16)
            sp.dma_start(far[:, 0:BLOCK_COLS].bitcast(i32), etype_cols[:, 0:BLOCK_COLS]).then_inc(edges_in, 16)
            sp.dma_start(xres, x_v).then_inc(x_in, 16)
            for to, w in ((w1, W1T), (w2, W2T), (wm, msgWT[0:F, :]), (wt, msgWT[F:F + ETD, :]), (wu, updWT)):
                sp.dma_start(to[:, :], w).then_inc(weights_in, 16)
            for k in range(K3):
                sp.dma_start(emb[:, k, :], embT).then_inc(weights_in, 16)
            for k, b in enumerate((b1, b2, msg_b, upd_b)):
                sp.dma_start(bias_in[:, k, :], b.partition_broadcast(K3)).then_inc(weights_in, 16)
            sp.dma_start(g_all[:, :], ln_g.partition_broadcast(P)).then_inc(weights_in, 16)
            sp.dma_start(b_all[:, :], ln_b.partition_broadcast(P)).then_inc(weights_in, 16)

            def store_codes(b, n):
                sp.wait_ge(code_T_ready, n)
                for k, to in enumerate((src_tab, type_tab)):
                    sp.dma_start(to[bass.ds(b, 1), :, :].rearrange("a t s -> (a t) s"), code_T[:, k * P:(k + 1) * P])\
                        .then_inc(code_T_stored, 16)

            def load_types(to, g, done):
                sp.dma_start(to, etype[bass.ds(g, 1), :, :].rearrange("a r e -> (a r) e")).then_inc(done, 16)

            def store_table(i, layer):
                for h in range(2):
                    if layer == 2:
                        sp.wait_ge(h_ready[h], i * 2 + (layer * 2 * STEPS + 1))
                    else:
                        sp.wait_ge(parts_ready[h], i + (layer * STEPS + 1))
                    sp.dma_start(tab_v[layer][:, tiles(i, h), :], oslot[h] if layer == 2 else htab[:, tiles(i, h), :])\
                        .then_inc(stored[h], 16)

            def load_rinv(i, layer, first=False):
                for h, (_, n) in enumerate(HALVES):
                    if not first:
                        sp.wait_ge(mean_ready[h], i * 2 + layer * 2 * STEPS if layer < 2 else i + 4 * STEPS)
                    sp.dma_start(rinv[h], one_row(rinv_tab)[:, nodes(i, h)].broadcast_to([P, n * P])).then_inc(rinv_loaded[h], 16)

            def load_all_rinv(layer):
                sp.wait_ge(added[4], (layer + 1) * B)
                loop(sp, STEPS, lambda i, first: load_rinv(i, layer, first), peel=True)

            def load_unit(layer, b, u):
                slots = len(UNITS[u]) * P
                for k, (tab_, to, parts) in enumerate(((src_tab, src_in, P), (type_tab, btypes_in, K3 * TYPES))):
                    if k == 0 or layer == 2:
                        sp.dma_start(to[u % 2][:, 0:slots],
                                     tab_[bass.ds(b, 1), UNITS[u][0]:UNITS[u][-1] + 1, :].rearrange("a t s -> a (t s)")
                                     .broadcast_to([parts, slots])).then_inc(src_loaded[u], 16)

            store_codes(0, 1)
            loop(sp, STEPS, lambda i, first: store_table(i, 0))
            for layer in range(LAYERS):
                def step(b, first):
                    c = Count(sp, layer, b, first, [(32, 32)] if layer == 0 else [])
                    for u in range(U):
                        if layer == 0:
                            sp.wait_ge(code_T_stored, c(32, 32))
                        if u >= 2 or not first or layer == 0:
                            if not (c.none and u < 2):
                                sp.wait_ge(src_hot_ready, c.unit(u - 2))
                            load_unit(layer, b, u)
                        if layer == 2 and u % 2 == 0:
                            gi = u // 2
                            if gi > 1 or not first:
                                sp.wait_ge(types_hot_ready[(gi + 2) % 4], b if gi < 2 else b + 1)
                            load_types(types_in[gi % 2], b * GROUPS_STEP + (FIRST_GROUP + gi), types_loaded[gi])
                        if layer == 1 and first and u == U - 1:
                            sp.dma_start(xres, x_v).then_inc(x_in, 16)
                        if layer == 0 and u == U - 1:
                            store_codes(b + 1, b + 2)
                loop(sp, B, step, peel=True)
                if layer < 2:
                    for u in range(2):
                        sp.wait_ge(src_hot_ready, (layer + 1) * B * U + u - 1)
                        load_unit(layer + 1, 0, u)

                if layer == 0:
                    sp.wait_ge(degree_ready, 1)
                    sp.dma_start(one_row(degree_tab), cnt[0:1, 0:TILES * P]).then_inc(degree_moved, 16)
                    sp.wait_ge(degree_moved, 16)
                    sp.dma_start(degree[:, :], degree_tab).then_inc(degree_moved, 16)
                    sp.wait_ge(degree_ready, 2)
                    sp.dma_start(rinv_tab, degree[:, :]).then_inc(degree_moved, 16)
                    sp.wait_ge(degree_moved, 48)
                    for i in range(3):
                        load_rinv(i, 0, i == 0)
                    with sp.Fori(3, STEPS) as i:
                        load_rinv(i, 0)
                        store_table(i - 3, 1)
                    for i in range(STEPS - 3, STEPS):
                        store_table(i, 1)
                elif layer == 1:
                    load_all_rinv(1)
                    loop(sp, STEPS, lambda i, first: store_table(i, 2))

            sp.wait_ge(far_known, 1)
            with sp.If(sp.value_load(flag[0:1, 0:1], min_val=0, max_val=P) > 0):
                sp.wait_ge(added[4], LAYERS * B)
                def fb_step(g, first):
                    if not first:
                        sp.wait_ge(fb_types_hot, g)
                    load_types(types_in[0], g, fb_types_in)
                loop(sp, GROUPS, fb_step, peel=True)

            load_all_rinv(2)

            def store_out(i, first):
                for h in range(2):
                    sp.wait_ge(out_ready[h], i + 1)
                    sp.dma_start(out_v[:, tiles(i, h), :], xres[:, tiles(i, h), :]).then_inc(out_stored[h], 16)
            loop(sp, STEPS, store_out)
            for h in range(2):
                sp.wait_ge(out_stored[h], 16 * STEPS)
            sp.wait_ge(code_T_stored, 32 * (B + 1))

        @block.gpsimd
        def _(pool):
            def iota(to, pattern, base, mult):
                nc.gpsimd.iota(to, pattern, base=base, channel_multiplier=mult,
                               allow_small_or_imprecise_dtypes=True).then_inc(consts, 1)
            iota(columns[:, :], [[1, P]], 0, 0)
            iota(columns_b[:, :], [[1, P]], 0, 0)
            iota(columns1_b[:, :], [[1, WIN_B]], 1, 0)
            iota(columns1[:, :], [[1, WIN_B]], 1, 0)
            iota(columns1_h[:, :], [[1, P]], 1, 0)
            iota(tile_cols[:, :], [[1, T]], 0, 0)
            iota(part_no[:, :], [[0, 1]], 0, 1)
            iota(part_i[:, 0:1], [[0, 1]], 0, 1)
            nc.gpsimd.memset(ones_b[:, :], 1.0).then_inc(consts, 1)
            nc.gpsimd.memset(eps[:, :], EPS).then_inc(consts, 1)
            nc.gpsimd.memset(ones[:, :], 1.0).then_inc(consts, 1)
            nc.gpsimd.memset(below[:, :], 1.0).then_inc(cleared, 1)
            nc.gpsimd.memset(ident[:, :], 0.0).then_inc(cleared, 1)
            pool.wait_ge(cleared, 2)
            nc.gpsimd.affine_select(out=ident[:, :], in_=ident[:, :], compare_op=ALU.not_equal, fill=1.0,
                                    base=0, pattern=[[-1, P]], channel_multiplier=1).then_inc(consts, 1)
            nc.gpsimd.affine_select(out=below[:, :], in_=below[:, :], compare_op=ALU.is_gt, fill=0.0,
                                    base=0, pattern=[[1, P]], channel_multiplier=-1).then_inc(consts, 1)

            def clear_sums(layer):
                for i in range(STEPS):
                    for h, (t0, n) in enumerate(HALVES):
                        at = (i * STEP + t0) * P
                        pool.wait_ge(mean_ready[h], i * 2 + (layer * 2 * STEPS + 1))
                        nc.gpsimd.memset(agg[:, at:at + n * P], 0.0).then_inc(sums_cleared, 1)
                nc.gpsimd.memset(agg[:, TILES * P:], 0.0).then_inc(sums_cleared, 1)

            def table_complete(layer):
                for h in range(2):
                    pool.wait_ge(stored[h], 16 * STEPS * (layer + 1))

            def gather(layer, to, cols, done):
                for c in range(C):
                    nc.gpsimd.indirect_dma_start(
                        out=to[:, c, :], out_offset=None, in_=tab[layer],
                        in_offset=bass.IndirectOffsetOnAxis(ap=cols[:, c:c + 1], axis=0)).then_inc(done, 16)

            nc.gpsimd.memset(agg[:, :], 0.0).then_inc(sums_cleared, 1)
            for layer in range(LAYERS):
                to = rows_f if layer == 2 else rows

                def step(b, first):
                    c = Count(pool, layer, b, first)
                    for gi in range(GROUPS_STEP):
                        table_complete(layer)
                        pool.wait_ge(idx_ready[gi], c.here())
                        if not (c.none and gi < 2):
                            pool.wait_ge(summed[(gi + 2) % 4], c.before() if gi < 2 else c.here())
                        gather(layer, to[gi % 2], idx[gi % 2], gathered[gi])
                        if c.none and gi == 1:
                            for h in range(2):
                                pool.wait_ge(h_ready[h], 2 * STEPS)
                            nc.gpsimd.memset(cnt, 0.0).then_inc(sums_cleared, 1)
                loop(pool, B, step, peel=layer == 0)

                if layer == 0:
                    pool.wait_ge(far_known, 1)
                    far_n = pool.value_load(flag[0:1, 0:1], min_val=0, max_val=P)
                with pool.If(far_n > 0):
                    def fb_step(g, first):
                        g1 = pool.snap(pool.to_reg(g + (layer * GROUPS + 1)))
                        table_complete(layer)
                        pool.wait_ge(fb_idx, g1)
                        gather(layer, to[0], fb_idx_cols, fb_gathered)
                    loop(pool, GROUPS, fb_step)
                if layer < 2:
                    clear_sums(layer)

            def residual(i, first):
                for h in range(2):
                    pool.wait_ge(scaled[h], i + 1)
                    here = xres[:, tiles(i, h), :]
                    nc.gpsimd.tensor_tensor(here, oslot[h], here, ALU.add).then_inc(out_ready[h], 1)
            loop(pool, STEPS, residual)

        @block.scalar
        def _(act):
            def normalise(i, h, to, func, inp, k):
                t0, n = HALVES[h]
                for j in range(n):
                    t = bass.ds(i * STEP + (t0 + j), 1)
                    last = nc.scalar.activation(to[h][:, j:j + 1, :], inp(j, t), func,
                                                bias=nmr[k][:, t], scale=rstd[k][:, t])
                return last

            def make_std(k):
                act.wait_ge(stats_ready, k)
                nc.scalar.activation(std[:, :], var[:, :], ACT.Sqrt, bias=eps[:, 0:1]).then_inc(std_ready, 1)
                act.wait_ge(norm_ready, k)

            def first_parts(i, h, layer, what, value):
                what.then_inc(h_ready[h], 1)
                act.wait_ge(h_ready[h], i * 2 + (layer * 2 * STEPS + 1))
                nc.scalar.activation(htab[:, tiles(i, h), part(0)], value[h], ACT.Copy).then_inc(h_ready[h], 1)

            def second_parts(i, layer):
                for h in range(2):
                    act.wait_ge(rest_h[h], i + (layer * STEPS + 1))
                    nc.scalar.activation(htab[:, tiles(i, h), part(1)], rslot[h], ACT.Copy).then_inc(second_h[h], 1)

            def table_steps(layer, step):
                step(0, True, False)
                with act.Fori(1, STEPS - 1) as i:
                    second_parts(i - 1, layer)
                    step(i, False, False)
                second_parts(STEPS - 2, layer)
                step(STEPS - 1, False, True)
                second_parts(STEPS - 1, layer)

            x_tiles = lambda j, t: xres[:, t, :]

            act.wait_ge(consts, CONSTS)
            make_std(1)

            def first_rows(i, first, last):
                for h in range(2):
                    first_parts(i, h, 0, normalise(i, h, hslot, ACT.Relu, x_tiles, 0), hslot)
            table_steps(0, first_rows)

            for layer in range(LAYERS):
                def step(b, first):
                    c = Count(act, layer, b, first, [(U, k - 2 * B * U) for k in range(-1, U + 1)] if layer == 2
                              else [(BUCKETS // R, k) for k in range(BUCKETS // R + 1)])
                    for u in range(U):
                        if layer < 2:
                            for j, t in enumerate(UNITS[u]):
                                act.wait_ge(pick_done[t % R], c.bucket(t))
                                nc.scalar.activation(picked[u % 2][:, j, :], pick_ps[t % 4], ACT.Copy)\
                                    .then_inc(pick_read[t % R], 1)
                            continue
                        act.wait_ge(unit_picked, c.unit(u, since=2))
                        if not (first and u < 2):
                            act.wait_ge(unit_summed, c.unit(u - 2))
                        m = len(UNITS[u])
                        nc.scalar.activation(messages[u % 2][:, 0:m, :], message_ps[u % 2][:, 0:m, :], ACT.Relu)\
                            .then_inc(messages_ready, 1)
                        if u in GROUP_HOT:
                            gi = GROUP_HOT.index(u)
                            act.wait_ge(pre_ready[gi], b + 1)
                            nc.scalar.activation(rows_f[gi % 2], rows_f[gi % 2], ACT.Relu).then_inc(msgs_ready[gi], 1)
                loop(act, B, step, peel=layer != 1)

                if layer == 2:
                    act.wait_ge(far_known, 1)
                    with act.If(act.value_load(flag[0:1, 0:1], min_val=0, max_val=P) > 0):
                        def fb_step(g, first):
                            act.wait_ge(fb_pre, g + 1)
                            nc.scalar.activation(rows_f[0], rows_f[0], ACT.Relu).then_inc(fb_msgs, 1)
                        loop(act, GROUPS, fb_step)

                def layer0_rows(i, first, last):
                    for h in range(2):
                        act.wait_ge(post_done[h], i + 1)
                        first_parts(i, h, 1, nc.scalar.activation(hslot[h], post_ps[h][:, 0:HALVES[h][1], :], ACT.Relu),
                                    hslot)

                def layer1_h(i, first):
                    for h in range(2):
                        if not first:
                            act.wait_ge(tr_done[h], i)
                        normalise(i, h, hslot, ACT.Relu, x_tiles, 1).then_inc(z_ready[h], 1)

                def layer1_rows(i, first, last):
                    if not last:
                        layer1_h(i + 1, False)
                    for h in range(2):
                        act.wait_ge(y_done[h], i + 1)
                        if not first:
                            act.wait_ge(stored[h], i * 16 + 16 * 2 * STEPS)
                        first_parts(i, h, 2, nc.scalar.activation(oslot[h], post_ps[h][:, 0:HALVES[h][1], :], ACT.Copy),
                                    oslot)
                if layer == 0:
                    table_steps(1, layer0_rows)
                elif layer == 1:
                    make_std(2)
                    layer1_h(0, True)
                    table_steps(2, layer1_rows)

            act.wait_ge(added[4], LAYERS * B)
            def input_again(i, first):
                for h in range(2):
                    if not first:
                        act.wait_ge(post_read[h], i + STEPS)
                    normalise(i, h, hslot, ACT.Relu, x_tiles, 1).then_inc(h_ready[h], 1)
            loop(act, STEPS, input_again, peel=True)
            make_std(3)

            def last_rows(i, first):
                for h in range(2):
                    if not first:
                        act.wait_ge(scaled[h], i)
                    normalise(i, h, rslot, ACT.Identity, lambda j, t: hres[:, t, :], 2).then_inc(z_ready[h], 1)
            loop(act, STEPS, last_rows, peel=True)

        @block.tensor
        def _(pe):
            def mm(to, left, right, start=True, stop=True):
                return nc.tensor.matmul(to, left, right, start=start, stop=stop)

            pe.wait_ge(weights_in, WEIGHT_LOADS)
            pe.wait_ge(consts, CONSTS)
            mm(setup_ps[0:K3 * TYPES, 0:F], emb[:, :, :].rearrange("e k t -> e (k t)"), wt[:, :]).then_inc(setup_done, 1)

            def window_sum(layer, s):
                for c in range(C):
                    if layer == 2:
                        last = mm(sum_ps[s], rows_f[s][:, c, :], hot[s][:, c, :], c == 0, c == C - 1)
                        continue
                    for k in range(K3):
                        last = mm(sum_ps[s], rows[s][:, c, part(k)], hot_b[s][:, c, :],
                                  (c, k) == (0, 0), (c, k) == (C - 1, K3 - 1))
                return last

            def window_count(s):
                for c in range(C):
                    mm(cnt_ps[s], ones_b[:, :], hot_b[s][:, c, :], c == 0, c == C - 1)

            def type_rows_of_group(s):
                for c in range(C):
                    last = mm(type_ps[:, c, :], types_hot[s][:, c * P:(c + 1) * P], type_rows[:, :])
                return last

            def sort_before(n, before):
                pe.wait_ge(in_tile_ready, n)
                if before is not None:
                    pe.wait_ge(code_T_ready, before)
                for c in range(BLOCK_C):
                    last = mm(before_ps, below[:, :], in_tile[:, :, c], c == 0, c == BLOCK_C - 1)
                last.then_inc(before_done, 1)

            def sort_table(n):
                pe.wait_ge(coded_ready, n)
                for c in range(BLOCK_C):
                    last = mm(table_ps, slot_hot[:, c, :], coded[:, :, c], c == 0, c == BLOCK_C - 1)
                last.then_inc(table_done, 1)

            def sort_turn(n):
                pe.wait_ge(consts, CONSTS)
                pe.wait_ge(code_f_ready, n)
                for k in range(2):
                    last = nc.tensor.transpose(code_T_ps[:, k * P:(k + 1) * P], code_f[:, k, :], ident[:, :])
                last.then_inc(code_T_done, 1)

            def pick(layer, c, u, j):
                t, slots = UNITS[u][j], slice(j * P, (j + 1) * P)
                left = src_hot[u % 2][:, slots]
                tile = t if t < TILES else bass.ds(c.first_tile + (t - TILES), 1)
                if layer < 2:
                    return mm(pick_ps[t % 4], left, htab[:, tile, :])
                to = message_ps[u % 2][:, j, :]
                for k in range(K3):
                    mm(to, left, htab[:, tile, part(k)], k == 0, False)
                return mm(to, btypes_hot[u % 2][:, slots], type_rows[:, :], False, True)

            def slot_sum(layer, u, j):
                t = UNITS[u][j]
                begin, end = t == 0, t == BUCKETS - 1
                if layer == 2:
                    return mm(bsum_ps, messages[u % 2][:, j, :], dst_hot_f[u % 2][:, j, :], begin, end)
                right = dst_hot[u % 2][:, j, :]
                if layer == 0:
                    mm(bcnt_ps, ones_b[:, :], right, begin, end)
                for k in range(K3):
                    last = mm(bsum_ps, picked[u % 2][:, j, part(k)], right, begin and k == 0, end and k == K3 - 1)
                return last

            sort_before(1, None)
            sort_table(1)
            sort_turn(1)
            far_n = None
            for layer in range(LAYERS):
                def unit(c, u):
                    if u < U:
                        pe.wait_ge(src_hot_ready, c.unit(u))
                    if u > 0:
                        pe.wait_ge(dst_hot_ready, c.unit(u - 1))
                    if u == 1 and not c.none:
                        pe.wait_ge(added[4], c.before())
                        if layer == 0:
                            pe.wait_ge(counted[4], c.before())
                    if layer == 2:
                        if u < U:
                            if not (c.first and u < 2):
                                pe.wait_ge(messages_ready, c.unit(u - 2, since=2))
                            for j in range(len(UNITS[u])):
                                last = pick(layer, c, u, j)
                            last.then_inc(unit_picked, 1)
                        if u > 0:
                            pe.wait_ge(messages_ready, c.unit(u - 1, since=2))
                            for j in range(len(UNITS[u - 1])):
                                last = slot_sum(layer, u - 1, j)
                            last.then_inc(unit_summed, 1)
                        return
                    for j in range(J):
                        if u < U and j < len(UNITS[u]):
                            t = UNITS[u][j]
                            if t >= 4 or not c.none:
                                pe.wait_ge(pick_read[(t - 4) % R], c.bucket(t - 4))
                            pick(layer, c, u, j).then_inc(pick_done[t % R], 1)
                        if u > 0 and j < len(UNITS[u - 1]):
                            t = UNITS[u - 1][j]
                            pe.wait_ge(pick_read[t % R], c.bucket(t))
                            last = slot_sum(layer, u - 1, j)
                    if u > 0:
                        last.then_inc(unit_summed, 1)

                def step(b, first):
                    c = Count(pe, layer, b, first, [
                        [(1, 2), (16 * C, 16 * C)] + [(BUCKETS // R, k) for k in range(BUCKETS // R + 1)],
                        [(16 * C, 16 * C)] + [(BUCKETS // R, k) for k in range(BUCKETS // R + 1)],
                        [(U, k - 2 * B * U) for k in range(-1, U + 1)]][layer])
                    c.first_tile = pe.value_load(first_tile[0:1, bass.ds(b * GROUPS_STEP, 1)], min_val=0,
                                                 max_val=TILES - SPILL)
                    for u in range(U):
                        gi = GROUP_AFTER.index(u) if u in GROUP_AFTER else None
                        unit(c, u)
                        if layer == 2 and u in GROUP_HOT:
                            gt = GROUP_HOT.index(u)
                            pe.wait_ge(types_hot_ready[gt], b + 1)
                            if gt > 0 or not first:
                                pe.wait_ge(pre_ready[(gt - 1) % 4], b if gt == 0 else b + 1)
                            type_rows_of_group(gt % 2).then_inc(types_done[gt], 1)
                        if layer == 0 and u == 1:
                            sort_before(SORT_N(c), c(1, 1))
                        if layer == 0 and u == 5:
                            sort_table(SORT_N(c))
                        if layer == 0 and u == 6:
                            sort_turn(SORT_N(c))
                        if gi is None:
                            continue
                        pe.wait_ge(hot_ready[gi], c.here())
                        if not (c.none and gi == 0):
                            seen_at = c.before() if gi == 0 else c.here()
                            pe.wait_ge(added[(gi + 3) % 4], seen_at)
                            if layer == 0:
                                pe.wait_ge(counted[(gi + 3) % 4], seen_at)
                        if layer == 0:
                            window_count(gi % 2)
                        if layer == 2:
                            pe.wait_ge(msgs_ready[gi], b + 1)
                        else:
                            pe.wait_ge(gathered[gi], c.here(16 * C))
                        window_sum(layer, gi % 2).then_inc(summed[gi], 1)
                    unit(c, U)
                if layer == 2:
                    pe.wait_ge(type_rows_ready, 1)
                for h in range(2):
                    pe.wait_ge(parts_ready[h], (layer + 1) * STEPS)
                loop(pe, B, step, peel=layer != 1)

                if layer == 0:
                    pe.wait_ge(far_ready, 1)
                    mm(setup_ps[0:1, F:F + 1], far_one[:, 0:1], ones[:, 0:1]).then_inc(setup_done, 1)
                    pe.wait_ge(far_known, 1)
                    far_n = pe.value_load(flag[0:1, 0:1], min_val=0, max_val=P)
                with pe.If(far_n > 0):
                    def fb_group(g, first):
                        if layer == 2:
                            pe.wait_ge(fb_types_hot, g + 1)
                            type_rows_of_group(0).then_inc(fb_types_done, 1)

                        def fb_window(w, first):
                            if layer == 2:
                                pe.wait_ge(fb_msgs, g + 1)
                            else:
                                pe.wait_ge(fb_gathered, g * (16 * C) + 16 * C * (layer * GROUPS + 1))
                            pe.wait_ge(fb_hot, g * WINDOWS + w + (layer * FB_ALL + 1))
                            if layer == 0:
                                window_count(0)
                            window_sum(layer, 0).then_inc(fb_summed, 1)
                        loop(pe, WINDOWS, fb_window)
                    loop(pe, GROUPS, fb_group)

                def node_products(h, left, weight, bias, bias_left):
                    for j in range(HALVES[h][1]):
                        at = slice(j * P, (j + 1) * P)
                        mm(post_ps[h][:, j, :], left[h][:, at], weight[:, :], True, False)
                        last = mm(post_ps[h][:, j, :], bias_left(h, at), bias_parts[:, bias, :], False, True)
                    return last

                def post(i, first):
                    for h in range(2):
                        pe.wait_ge(mean_ready[h], i * 2 + (layer * 2 * STEPS + 2) if layer < 2
                                   else i + (4 * STEPS + 1))
                        if layer == 0 and not first:
                            pe.wait_ge(h_ready[h], i * 2 + (2 * STEPS - 1))
                        if layer > 0 and not first:
                            pe.wait_ge(post_read[h], i + (layer - 1) * STEPS)
                        weight, bias = ((w1, 0), (w2, 1), (wu, 3))[layer]
                        node_products(h, mean_T, weight, bias,
                                      (lambda h, at: has_in[h][:, at]) if layer < 2 else (lambda h, at: ones_b[0:K3, :]))\
                            .then_inc(post_done[h], 1)
                loop(pe, STEPS, post, peel=True)

                if layer == 1:
                    def source_part(i, first):
                        for h, (_, n) in enumerate(HALVES):
                            pe.wait_ge(z_ready[h], i + 1)
                            if not first:
                                pe.wait_ge(tr_read[h], i)
                            for j in range(n):
                                last = nc.tensor.transpose(tr_ps[h][:, j * P:(j + 1) * P], hslot[h][:, j, :], ident[:, :])
                            last.then_inc(tr_done[h], 1)
                        for h in range(2):
                            pe.wait_ge(tr_read[h], i + 1)
                            if not first:
                                pe.wait_ge(h_ready[h], i * 2 + (4 * STEPS - 1))
                            node_products(h, mean_T, wm, 2, lambda h, at: ones_b[0:K3, :]).then_inc(y_done[h], 1)
                    loop(pe, STEPS, source_part, peel=True)

        @block.vector
        def _(dve):
            steps = Steps(dve)
            V = nc.vector

            def chained(*instructions):
                for make in instructions:
                    steps.done(make())
                    steps.wait()

            def tile_stats(source, i, h):
                t0, n = HALVES[h]
                for j in range(n):
                    t = bass.ds(i * STEP + (t0 + j), 1)
                    last = V.bn_stats(stats[:, t, :], source[:, t, :])
                return last

            def mean_and_var():
                steps.wait()
                steps.done(V.tensor_tensor(mean[:, :], stats[:, :, 1], stats[:, :, 4], ALU.add))
                steps.done(V.tensor_tensor(std[:, :], stats[:, :, 1], stats[:, :, 4], ALU.subtract))
                steps.done(V.tensor_tensor(var[:, :], stats[:, :, 2], stats[:, :, 5], ALU.add))
                steps.wait()
                steps.done(V.tensor_single_scalar(mean[:, :], mean[:, :], 0.5, op=ALU.mult))
                steps.done(V.scalar_tensor_tensor(out=std[:, :], in0=std[:, :], scalar=0.25, in1=std[:, :],
                                                  op0=ALU.mult, op1=ALU.mult))
                steps.wait()
                V.scalar_tensor_tensor(out=var[:, :], in0=var[:, :], scalar=1.0 / F, in1=std[:, :],
                                       op0=ALU.mult, op1=ALU.add).then_inc(stats_ready, 1)

            def make_norm(k):
                dve.wait_ge(std_ready, k + 1)
                chained(lambda: V.reciprocal(rstd[k][:, :], std[:, :]))
                V.scalar_tensor_tensor(out=nmr[k][:, :], in0=mean[:, :], scalar=-1.0, in1=rstd[k][:, :],
                                       op0=ALU.mult, op1=ALU.mult).then_inc(norm_ready, 1)

            def rests(i, layer, value, first=False):
                for h in range(2):
                    dve.wait_ge(h_ready[h], i * 2 + (layer * 2 * STEPS + 2))
                    if not (first and layer == 0):
                        dve.wait_ge(parts_ready[h], i + layer * STEPS)
                    V.tensor_tensor(rslot[h], value[h], htab[:, tiles(i, h), part(0)], ALU.subtract).then_inc(rest_h[h], 1)

            def third_parts(i, layer):
                for h in range(2):
                    dve.wait_ge(second_h[h], i + (layer * STEPS + 1))
                    V.tensor_tensor(htab[:, tiles(i, h), part(2)], rslot[h], htab[:, tiles(i, h), part(1)], ALU.subtract)\
                        .then_inc(parts_ready[h], 1)

            def table_steps(layer, step, value):
                step(0, True)
                step(1, False)
                rests(0, layer, value, True)
                with dve.Fori(2, STEPS) as i:
                    step(i, False)
                    third_parts(i - 2, layer)
                    rests(i - 1, layer, value)
                third_parts(STEPS - 2, layer)
                rests(STEPS - 1, layer, value)
                third_parts(STEPS - 1, layer)

            def split_over_partitions(value, p0, p1, p2, f0, f1, mask, to):
                chained(lambda: V.tensor_copy(p0, value),
                        lambda: V.tensor_tensor(f0, value, p0, ALU.subtract),
                        lambda: V.tensor_copy(p1, f0),
                        lambda: V.tensor_tensor(p2, f0, p1, ALU.subtract),
                        lambda: V.tensor_scalar(f0, p0, mask[:, 0:1], None, ALU.mult),
                        lambda: V.scalar_tensor_tensor(out=f1, in0=p1, scalar=mask[:, 1:2], in1=f0,
                                                       op0=ALU.mult, op1=ALU.add))
                return V.scalar_tensor_tensor(out=to, in0=p2, scalar=mask[:, 2:3], in1=f1, op0=ALU.mult, op1=ALU.add)

            dve.wait_ge(edges_in, EDGE_LOADS)
            for s in range(2):
                V.tensor_copy(idx[s][:, :], src_all[:, (FIRST_GROUP + s) * C:(FIRST_GROUP + s + 1) * C])\
                    .then_inc(idx_ready[s], 1)
            per_group = lambda a: a[:, :].rearrange("p (g c) -> p g c", c=C)
            steps.done(V.tensor_tensor(per_group(rel), per_group(dst_all),
                                       base_all[:, :].unsqueeze(2).broadcast_to([P, GROUPS, C]), ALU.subtract))
            int_a, int_b = region_b[:, 0:BLOCK_COLS].bitcast(i32), region_b[:, BLOCK_COLS:2 * BLOCK_COLS].bitcast(i32)
            float_c = region_b[:, 2 * BLOCK_COLS:3 * BLOCK_COLS]
            types_i = far[:, 0:BLOCK_COLS].bitcast(i32)
            block_src, block_rel = src_all[:, 0:BLOCK_COLS], rel[:, 0:BLOCK_COLS]
            chained(lambda: V.tensor_single_scalar(first_tile[:, :], base_all[:, :], 7, op=ALU.arith_shift_right),
                    lambda: V.tensor_single_scalar(first_tile[:, :], first_tile[:, :], TILES - SPILL, op=ALU.min),
                    lambda: V.tensor_single_scalar(int_a, block_src, 7, op=ALU.arith_shift_right),
                    lambda: V.tensor_copy(tile_no[:, :], int_a),
                    lambda: V.tensor_single_scalar(int_a, block_src, P - 1, op=ALU.bitwise_and),
                    lambda: V.tensor_single_scalar(int_b, types_i, 7, op=ALU.logical_shift_left),
                    lambda: V.tensor_tensor(int_a, int_a, int_b, ALU.add),
                    lambda: V.tensor_copy(codes[:, 0, :], int_a),
                    lambda: V.tensor_single_scalar(float_c, block_rel, 0.0, op=ALU.is_ge),
                    lambda: V.scalar_tensor_tensor(out=float_c, in0=block_rel, scalar=float(WIN_B - 1), in1=float_c,
                                                   op0=ALU.is_le, op1=ALU.mult),
                    lambda: V.scalar_tensor_tensor(out=codes[:, 1, :], in0=block_rel, scalar=1.0, in1=float_c,
                                                   op0=ALU.add, op1=ALU.mult),
                    lambda: V.memset(scan_mask, 1.0),
                    lambda: V.memset(scan_mask[:, :, 0:1], 0.0))

            flat = lambda a: a.rearrange("p t c -> p (t c)")

            def sort_tiles(b):
                V.tensor_tensor(in_tile, tile_cols[:, :].unsqueeze(2).broadcast_to([P, T, BC]),
                                tile_no[:, bass.ds(b * BC, BC)].unsqueeze(1).broadcast_to([P, T, BC]), ALU.is_equal)\
                    .then_inc(in_tile_ready, 1)

            def sort_scan(n):
                dve.wait_ge(in_tile_ready, n)
                steps.done(V.tensor_tensor_scan(flat(seen), flat(scan_mask), flat(in_tile), 0.0, ALU.mult, ALU.add))

            def sort_before_tiles(n):
                dve.wait_ge(before_done, n)
                steps.wait()
                chained(lambda: V.tensor_tensor(prod, seen, before_ps.unsqueeze(2).broadcast_to([P, T, BC]), ALU.add))
                steps.done(V.tensor_tensor(prod, prod, in_tile, ALU.mult))

            def sort_ranks(b):
                steps.wait()
                chained(lambda: V.tensor_reduce(out=rank1[:, bass.ds(b * BC, BC)], in_=prod.rearrange("p t c -> p c t"),
                                                axis=AX.X, op=ALU.add))

            def sort_codes(b, k, own=None):
                rank = rank1[:, bass.ds(b * BC, BC)]
                near, beyond, spill, slot = (sort_small[:, i, :] for i in range(4))
                two = lambda a: a.unsqueeze(1).broadcast_to([P, 2, BC])
                if k == 0:
                    steps.done(V.tensor_single_scalar(near, rank, float(P), op=ALU.is_le))
                    steps.done(V.tensor_single_scalar(beyond, rank, float(P), op=ALU.is_gt))
                    steps.wait()
                    steps.done(V.scalar_tensor_tensor(out=spill, in0=rank, scalar=float(2 * P), in1=beyond,
                                                      op0=ALU.is_le, op1=ALU.mult))
                    steps.done(V.tensor_tensor(split_codes[0], codes[:, :, bass.ds(b * BC, BC)], two(near), ALU.mult))
                    steps.wait()
                    steps.done(V.tensor_tensor(split_codes[1], codes[:, :, bass.ds(b * BC, BC)], two(spill), ALU.mult))
                    steps.done(V.scalar_tensor_tensor(out=slot, in0=spill, scalar=float(-P), in1=rank,
                                                      op0=ALU.mult, op1=ALU.add))
                    steps.wait()
                    own = dve.value_load(first_tile[0:1, bass.ds(b * GROUPS_STEP, 1)], min_val=0, max_val=TILES - SPILL)
                for at, m, code, tiles_of in ((k * BUCKETS, T, split_codes[0], in_tile),
                                              (k * BUCKETS + T, SPILL, split_codes[1], in_tile[:, bass.ds(own, SPILL), :])):
                    V.tensor_tensor(coded[:, at:at + m, :], tiles_of,
                                    code[:, k, :].unsqueeze(1).broadcast_to([P, m, BC]), ALU.mult)
                if k == 1:
                    V.tensor_tensor(slot_hot, columns1_h[:, :].unsqueeze(1).broadcast_to([P, BC, P]),
                                    slot.unsqueeze(2).broadcast_to([P, BC, P]), ALU.is_equal).then_inc(coded_ready, 1)
                return own

            def sort_slots(b, n):
                dve.wait_ge(table_done, n)
                M = BUCKETS
                steps.done(V.tensor_copy(slot_dst[:, bass.ds(b * M, M)], table_ps[:, M:2 * M]))
                chained(lambda: V.tensor_copy(code_i[:, 0:M], table_ps[:, 0:M]),
                        lambda: V.tensor_single_scalar(code_i[:, M:2 * M], code_i[:, 0:M], P - 1, op=ALU.bitwise_and),
                        lambda: V.tensor_single_scalar(code_i[:, 2 * M:3 * M], code_i[:, 0:M], 7, op=ALU.arith_shift_right))
                V.tensor_copy(code_f, code_i[:, M:3 * M].rearrange("p (k t) -> p k t", k=2)).then_inc(code_f_ready, 1)

            def sort_turned(b, n, stored_before):
                dve.wait_ge(code_T_done, n)
                if stored_before is not None:
                    dve.wait_ge(code_T_stored, stored_before)
                V.tensor_copy(code_T, code_T_ps).then_inc(code_T_ready, 1)
            SORT_STEPS = 1 + 3 + 6 + 4

            dve.wait_ge(consts, CONSTS)
            sort_tiles(0)

            dve.wait_ge(x_in, 16)
            for i in range(STEPS):
                for h in range(2):
                    steps.done(tile_stats(xres, i, h))
            mean_and_var()
            sort_scan(1)
            make_norm(0)

            own = None
            for i in range(STEPS + 2):
                if i == 2:
                    sort_before_tiles(1)
                elif i == 3:
                    sort_ranks(0)
                    own = sort_codes(0, 0)
                elif i == 4:
                    sort_codes(0, 1, own)
                elif i == 5:
                    sort_slots(0, 1)
                elif i == 6:
                    sort_turned(0, 1, None)
                if i > 1:
                    third_parts(i - 2, 0)
                if 0 < i <= STEPS:
                    rests(i - 1, 0, hslot, i == 1)

            chained(lambda: V.tensor_single_scalar(part_i[:, 1:2], part_i[:, 0:1], 4, op=ALU.arith_shift_right),
                    lambda: V.tensor_copy(third[:, :], part_i[:, 1:2]),
                    lambda: V.tensor_single_scalar(part_i[:, 1:2], part_i[:, 0:1], TYPES - 1, op=ALU.bitwise_and),
                    lambda: V.tensor_copy(type_no[:, :], part_i[:, 1:2]))
            for k in range(K3):
                steps.done(V.tensor_single_scalar(masks[:, k:k + 1], third[:, :], float(k), op=ALU.is_equal))
            dve.wait_ge(setup_done, 1)
            product = setup_ps[0:K3 * TYPES, 0:F]
            split_over_partitions(product, type_p[:, 0, :], type_p[:, 1, :], type_p[:, 2, :], type_f[:, 0, :],
                                  type_f[:, 1, :], masks, type_rows[:, :]).then_inc(type_rows_ready, 1)

            def make_hot(layer, s, cols):
                to = hot[s][:, :, :] if layer == 2 else hot_b[s]
                return V.tensor_tensor(to, (columns if layer == 2 else columns_b)[:, :].unsqueeze(1).broadcast_to([P, C, P]),
                                       cols.unsqueeze(2).broadcast_to([P, C, P]), ALU.is_equal)

            def make_types_hot(s):
                return V.tensor_scalar(types_hot[s], types_in[s], type_no[:, 0:1], None, ALU.is_equal)

            far_n = None
            for layer in range(LAYERS):
                def window_add(n, at, size, ps, cps, before):
                    base = dve.value_load(base_all[0:1, bass.ds(at, 1)], min_val=0, max_val=N)
                    window = bass.ds(base, size)
                    if before is not None:
                        dve.wait_ge(added[n - 1], before)
                    V.tensor_tensor(agg[:, window], agg[:, window], ps, ALU.add).then_inc(added[n], 1)
                    if layer == 0:
                        if before is not None:
                            dve.wait_ge(counted[n - 1], before)
                        V.tensor_tensor(cnt[:, window], cnt[:, window], cps, ALU.add).then_inc(counted[n], 1)

                def group_add(gi, b, count, before):
                    dve.wait_ge(summed[gi], count)
                    window_add(gi, b * GROUPS_STEP + (FIRST_GROUP + gi), WIN_G, sum_ps[gi % 2], cnt_ps[gi % 2], before)

                def last_adds(b, count, unit):
                    group_add(3, b, count, count)
                    dve.wait_ge(unit_summed, unit)
                    window_add(4, b * GROUPS_STEP, WIN_B, bsum_ps, bcnt_ps, count)

                cleared_at = 2 if layer == 0 else 2 + layer * (2 * STEPS + 1)

                def main(b, first):
                    c = Count(dve, layer, b, first, [(16, 16), (16 * C, 16 * C)] + [
                        [(1, 2), (32, 32)] + [(BUCKETS // R, k) for k in range(BUCKETS // R + 1)],
                        [(BUCKETS // R, k) for k in range(BUCKETS // R + 1)],
                        [(32, 32 - 2 * B * 16)] + [(U, k - 2 * B * U) for k in range(-1, U + 1)]][layer])

                    def source_hot(u):
                        dve.wait_ge(src_loaded[u], c.here(16) if layer < 2 else c(32, 32 - 2 * B * 16))
                        s, m = u % 2, len(UNITS[u])
                        if layer == 2 and not (first and u < 2):
                            dve.wait_ge(unit_picked, c.unit(u - 2, since=2))
                        elif layer < 2 and not (c.none and u < 2):
                            t = UNITS[u - 2][-1] - (0 if u >= 2 else BUCKETS)
                            dve.wait_ge(pick_done[t % R], c.bucket(t))
                        if layer == 2:
                            V.tensor_scalar(btypes_hot[s][:, 0:m * P], btypes_in[s][:, 0:m * P], type_no[:, 0:1], None,
                                            ALU.is_equal)
                        V.tensor_scalar(src_hot[s][:, 0:m * P], src_in[s][:, 0:m * P], part_no[:, 0:1], None, ALU.is_equal)\
                            .then_inc(src_hot_ready, 1)

                    def destination_hot(u):
                        if not (c.none and u < 2):
                            dve.wait_ge(unit_summed, c.unit(u - 2))
                        to, numbers = (dst_hot_f, columns1) if layer == 2 else (dst_hot, columns1_b)
                        for j, t in enumerate(UNITS[u]):
                            last = V.tensor_scalar(to[u % 2][:, j, :], numbers[:, :],
                                                   slot_dst[:, bass.ds(b * BUCKETS + t, 1)], None, ALU.is_equal)
                        last.then_inc(dst_hot_ready, 1)

                    def group_hot(gi):
                        g = b * GROUPS_STEP + (FIRST_GROUP + gi)
                        if not (c.none and gi < 2):
                            dve.wait_ge(summed[(gi + 2) % 4], c.before() if gi < 2 else c.here())
                        make_hot(layer, gi % 2, rel[:, bass.ds(g * C, C)]).then_inc(hot_ready[gi], 1)
                        if layer == 2:
                            dve.wait_ge(types_loaded[gi], b * 16 + 16)
                            if gi > 1 or not first:
                                dve.wait_ge(types_done[(gi + 2) % 4], b if gi < 2 else b + 1)
                            make_types_hot(gi % 2).then_inc(types_hot_ready[gi], 1)

                    def group_rows(gi):
                        g = b * GROUPS_STEP + (FIRST_GROUP + gi)
                        dve.wait_ge(gathered[gi], c.here(16 * C))
                        V.tensor_copy(idx[gi % 2][:, :], src_all[:, bass.ds((g + 2) * C, C)])\
                            .then_inc(idx_ready[(gi + 2) % 4], 1)
                        if layer == 2:
                            dve.wait_ge(types_done[gi], b + 1)
                            V.tensor_tensor(rows_f[gi % 2], type_ps, rows_f[gi % 2], ALU.add).then_inc(pre_ready[gi], 1)

                    source_hot(0)
                    for u in range(U):
                        if u + 1 < U:
                            source_hot(u + 1)
                        if u in GROUP_HOT and (layer == 2 or u > 0):
                            group_hot(GROUP_HOT.index(u))
                        destination_hot(u)
                        if u == 0 and not first:
                            last_adds(b - 1, c.before(), c.unit(U - 1, last_step=True))
                        if u == 0 and layer < 2:
                            group_hot(0)
                        if layer == 0:
                            n = SORT_N(c)
                            if u == 0:
                                sort_tiles(b + 1)
                            elif u == 1:
                                sort_scan(n)
                            elif u == 2:
                                sort_before_tiles(n)
                            elif u == 3:
                                sort_ranks(b + 1)
                                own = sort_codes(b + 1, 0)
                            elif u == 4:
                                sort_codes(b + 1, 1, own)
                            elif u == 6:
                                sort_slots(b + 1, n)
                            elif u == 7:
                                sort_turned(b + 1, n, c(32, 32))
                        if u in rows_at:
                            group_rows(rows_at.index(u))
                        if u - 1 in GROUP_AFTER[:3]:
                            gi = GROUP_AFTER.index(u - 1)
                            if first and gi == 0:
                                dve.wait_ge(sums_cleared, cleared_at)
                            group_add(gi, b, c.here(), None if c.none and gi == 0 else c.before() if gi == 0 else c.here())
                rows_at = GROUP_HOT if layer == 2 else GROUP_AFTER
                if layer == 0:
                    steps.loop(B, SORT_STEPS, main, peel=True)
                else:
                    loop(dve, B, main, peel=True)
                if layer == 0:
                    mask = region_b[:, 0:GROUPS * C]
                    spare = region_b[:, GROUPS * C:GROUPS * C + B * BC]
                    halves = ((slice(0, B * BC), WIN_B), (slice(B * BC, GROUPS * C), WIN_G))
                    steps.wait()
                    chained(lambda: V.tensor_single_scalar(mask, rel[:, :], 0.0, op=ALU.is_lt))
                    for at, size in halves:
                        steps.done(V.scalar_tensor_tensor(out=far[:, at], in0=rel[:, at], scalar=float(size - 1),
                                                          in1=mask[:, at], op0=ALU.is_gt, op1=ALU.max))
                    steps.wait()
                    at = halves[0][0]
                    own = mask[:, at].rearrange("p (g c) -> p g c", c=C)
                    in_block = lambda a: a[:, at]
                    chained(lambda: V.scalar_tensor_tensor(out=far[:, at], in0=rank1[:, at], scalar=float(2 * P),
                                                           in1=far[:, at], op0=ALU.is_gt, op1=ALU.max),
                            lambda: V.tensor_tensor(own, in_block(tile_no).rearrange("p (g c) -> p g c", c=C),
                                                    first_tile[:, 0:B * GROUPS_STEP].unsqueeze(2)
                                                    .broadcast_to([P, B * GROUPS_STEP, C]), ALU.subtract),
                            lambda: V.tensor_single_scalar(spare, mask[:, at], 0.0, op=ALU.is_lt),
                            lambda: V.scalar_tensor_tensor(out=spare, in0=mask[:, at], scalar=float(SPILL - 1), in1=spare,
                                                           op0=ALU.is_gt, op1=ALU.max),
                            lambda: V.scalar_tensor_tensor(out=spare, in0=rank1[:, at], scalar=float(P), in1=spare,
                                                           op0=ALU.is_gt, op1=ALU.mult),
                            lambda: V.tensor_tensor(far[:, at], far[:, at], spare, ALU.max),
                            lambda: V.scalar_tensor_tensor(out=mask, in0=dst_all[:, :], scalar=1.0, in1=far[:, :],
                                                           op0=ALU.add, op1=ALU.mult),
                            lambda: V.tensor_single_scalar(far[:, :], mask, -1.0, op=ALU.add),
                            lambda: V.reduce_max(far_max[:, :], far[:, :], axis=AX.X))
                    V.tensor_single_scalar(far_one[:, :], far_max[:, :], 0.0, op=ALU.is_ge).then_inc(far_ready, 1)
                last_adds(B - 1, (layer + 1) * B, (layer + 1) * B * U)
                dve.wait_ge(added[4], (layer + 1) * B)
                dve.wait_ge(counted[4], B)
                if layer == 0:
                    dve.wait_ge(setup_done, 2)
                    V.tensor_copy(flag[0:1, 0:1], setup_ps[0:1, F:F + 1]).then_inc(far_known, 1)
                    dve.wait_ge(far_known, 1)
                    far_n = dve.value_load(flag[0:1, 0:1], min_val=0, max_val=P)

                with dve.If(far_n > 0):
                    ADDS = 3 * WINDOWS + 1

                    def fb_group(g, first):
                        V.tensor_copy(fb_idx_cols[:, :], src_all[:, bass.ds(g * C, C)]).then_inc(fb_idx, 1)
                        if layer == 2:
                            dve.wait_ge(fb_types_in, g * 16 + 16)
                            make_types_hot(0).then_inc(fb_types_hot, 1)
                        dve.wait_ge(fb_gathered, g * (16 * C) + 16 * C * (layer * GROUPS + 1))
                        if layer == 2:
                            dve.wait_ge(fb_types_done, g + 1)
                            V.tensor_tensor(rows_f[0], type_ps, rows_f[0], ALU.add).then_inc(fb_pre, 1)
                        V.tensor_copy(far_w[:, :], far[:, bass.ds(g * C, C)]).then_inc(fb_added, 1)

                        def fb_window(w, first):
                            at = g * WINDOWS + w + (layer * FB_ALL + 1)
                            dve.wait_ge(fb_added, g * ADDS + w * 3 + (layer * ADDS * GROUPS + 1))
                            make_hot(layer, 0, far_w[:, :]).then_inc(fb_hot, 1)
                            dve.wait_ge(fb_hot, at)
                            V.tensor_single_scalar(far_w[:, :], far_w[:, :], float(-P), op=ALU.add).then_inc(fb_added, 1)
                            dve.wait_ge(fb_summed, at)
                            window = bass.ds(w * P, P)
                            V.tensor_tensor(agg[:, window], agg[:, window], sum_ps[0], ALU.add).then_inc(fb_added, 1)
                            if layer == 0:
                                V.tensor_tensor(cnt[:, window], cnt[:, window], cnt_ps[0], ALU.add).then_inc(fb_added, 1)
                            else:
                                dve.engine_nop().then_inc(fb_added, 1)
                        loop(dve, WINDOWS, fb_window)
                    loop(dve, GROUPS, fb_group)
                    dve.wait_ge(fb_added, (layer + 1) * ADDS * GROUPS)

                if layer == 0:
                    dve.engine_nop().then_inc(degree_ready, 1)
                    dve.wait_ge(weights_in, WEIGHT_LOADS)
                    for k in range(K3):
                        steps.done(V.tensor_single_scalar(bias_masks[:, k:k + 1], part_no[0:K3, :], float(k), op=ALU.is_equal))
                    steps.wait()
                    steps.done(split_over_partitions(bias_in[:, :, :], *bias_p, *bias_f, bias_masks,
                                                     bias_parts[:, :, :]))
                    steps.wait()
                    dve.wait_ge(degree_moved, 32)
                    chained(lambda: V.tensor_single_scalar(at_least_1[:, :], degree[:, :], 1.0, op=ALU.max),
                            lambda: V.reciprocal(at_least_1[:, :], at_least_1[:, :]))
                    V.scalar_tensor_tensor(out=degree[:, :], in0=degree[:, :], scalar=1.0, in1=at_least_1[:, :],
                                           op0=ALU.min, op1=ALU.mult).then_inc(degree_ready, 1)

                def means(i, first):
                    for h in range(2):
                        at = nodes(i, h)
                        if layer == 2 and first:
                            dve.wait_ge(y_done[h], STEPS)
                        elif layer > 0 or not first:
                            dve.wait_ge(post_done[h], i + layer * STEPS)
                        dve.wait_ge(rinv_loaded[h], i * 16 + 16 * (layer * STEPS + 1))
                        V.tensor_tensor(mean_T[h], agg[:, at], rinv[h], ALU.mult).then_inc(mean_ready[h], 1)
                        if layer < 2:
                            V.tensor_single_scalar(has_in[h], rinv[h][0:K3, :], 0.0, op=ALU.is_gt).then_inc(mean_ready[h], 1)

                def residual(i):
                    to = xres if layer == 1 else hres
                    for h, (_, n) in enumerate(HALVES):
                        dve.wait_ge(post_done[h], i + (layer * STEPS + 1))
                        if layer == 2:
                            dve.wait_ge(h_ready[h], i + (6 * STEPS + 1))
                        V.tensor_tensor(to[:, tiles(i, h), :], post_ps[h][:, 0:n, :],
                                        xres[:, tiles(i, h), :] if layer == 1 else hslot[h], ALU.add).then_inc(post_read[h], 1)
                        dve.wait_ge(post_read[h], i + ((layer - 1) * STEPS + 1))
                        steps.done(tile_stats(to, i, h))

                if layer == 0:
                    table_steps(1, means, hslot)
                    continue
                dve.wait_ge(x_in, 32)
                means(0, True)
                with dve.Fori(1, STEPS) as i:
                    means(i, False)
                    residual(i - 1)
                steps.n += 2 * (STEPS - 2)
                residual(STEPS - 1)
                mean_and_var()
                make_norm(layer)

                if layer == 1:
                    def transposed(i, first):
                        for h, (_, n) in enumerate(HALVES):
                            dve.wait_ge(tr_done[h], i + 1)
                            if not first:
                                dve.wait_ge(y_done[h], i)
                            V.tensor_copy(mean_T[h], tr_ps[h][:, 0:n * P]).then_inc(tr_read[h], 1)
                    table_steps(2, transposed, oslot)
                else:
                    def scale(i, first):
                        for h, (_, n) in enumerate(HALVES):
                            V.tensor_tensor(xres[:, tiles(i, h), :], xres[:, tiles(i, h), :],
                                            b_all[:, :].unsqueeze(1).broadcast_to([P, n, F]), ALU.add)
                            dve.wait_ge(z_ready[h], i + (STEPS + 1))
                            if not first:
                                dve.wait_ge(out_ready[h], i)
                            V.tensor_tensor(oslot[h], rslot[h], g_all[:, :].unsqueeze(1).broadcast_to([P, n, F]), ALU.mult)\
                                .then_inc(scaled[h], 1)
                    loop(dve, STEPS, scale, peel=True)


def kernel(**inputs):
    import numpy as np
    import concourse.bacc as bacc
    from concourse import mybir
    from concourse.bass_utils import run_bass_kernel_spmd

    a = {k: np.ascontiguousarray(v) for k, v in inputs.items()}
    N, F = a["x"].shape
    E = a["src"].shape[0]
    assert (GROUPS - 1) * GE < E <= GROUPS * GE
    rows = -(-N // P) * P
    types = a["L1_gnn_edge_emb_W"].shape[0]

    def padded(e, fill):
        return np.concatenate([e.astype(np.int32), np.full(GROUPS * GE - E, fill, np.int32)])

    def by_partition(e):
        return np.ascontiguousarray(e.reshape(GROUPS * C, P).T)

    dst = padded(a["dst"], N)
    etype = padded(a["edge_type_16"], 0)
    blocks = GROUPS // 2
    firsts = np.arange(GROUPS)
    firsts = np.where(firsts < blocks, firsts // GROUPS_STEP * GROUPS_STEP, firsts) * GE
    arrays = {
        "x": np.concatenate([a["x"], np.zeros((rows - N, F), a["x"].dtype)]),
        "src": by_partition(padded(a["src"], 0)),
        "dst": by_partition(dst),
        "first_dst": dst[firsts],
        "etype_cols": by_partition(etype),
        "etype": np.broadcast_to(etype.reshape(GROUPS, 1, GE), (GROUPS, 3 * types, GE)),
        "W1T": a["L0_gnn_W1"].T, "b1": a["L0_gnn_b1"], "W2T": a["L0_gnn_W2"].T, "b2": a["L0_gnn_b2"],
        "embT": a["L1_gnn_edge_emb_W"].T, "msgWT": a["L1_gnn_msg_W"].T, "msg_b": a["L1_gnn_msg_b"],
        "updWT": a["L1_gnn_upd_W"].T, "upd_b": a["L1_gnn_upd_b"], "ln_g": a["L1_gnn_ln_g"], "ln_b": a["L1_gnn_ln_b"],
    }
    arrays = {k: np.ascontiguousarray(v) for k, v in arrays.items()}
    nc = bacc.Bacc("TRN2", target_bir_lowering=False, num_devices=1)
    args = {k: nc.dram_tensor(f"in_{k}", v.shape, mybir.dt.from_np(v.dtype), kind="ExternalInput").ap()
            for k, v in arrays.items()}
    out = nc.dram_tensor("out_dram", (rows, F), mybir.dt.float32, kind="ExternalOutput").ap()
    gnn_program(nc, N, **args, out=out)
    r = run_bass_kernel_spmd(nc, [{f"in_{k}": v for k, v in arrays.items()}], core_ids=[0])
    return r.results[0]["out_dram"][:N]
```
